# Optimizing a Trainium2 kernel written in Bass

```python
import numpy as np
import jax
import jax.numpy as jnp

def _softmax(x, axis=-1):
    return jax.nn.softmax(x, axis=axis)

def _gelu(x):
    return jax.nn.gelu(x, approximate=True)

def _silu(x):
    return jax.nn.silu(x)

def _sigmoid(x):
    return jax.nn.sigmoid(x)

def _layernorm(x, axis=-1, eps=1e-05):
    m = jnp.mean(x, axis=axis, keepdims=True)
    v = jnp.var(x, axis=axis, keepdims=True)
    return (x - m) / jnp.sqrt(v + eps)

def _scatter_add(tgt, idx, src, axis=0):
    return tgt.at[idx].add(src)

def _segment_sum(src, seg, n):
    return jax.ops.segment_sum(src, seg, n)
kernel_name = 'mk_xattn_seq_d1_seqx_r4_0bd340'

def setup_inputs(seed: int=0):
    np.random.seed(seed)
    _w = jnp.asarray

    def _rec_inputs():
        import jax
        import jax.numpy as jnp
        _rk = jax.random.key(seed)
        x = -0.0002928 + 1 * jax.random.normal(jax.random.fold_in(_rk, 1), (8, 112, 256), jnp.float32)
        _lenS = 112 - jax.random.randint(jax.random.fold_in(_rk, 7), (8,), 0, max(1, 112 // 4) + 1, jnp.int32)
        _lenS2 = 375 - jax.random.randint(jax.random.fold_in(_rk, 8), (8,), 0, max(1, 375 // 4) + 1, jnp.int32)
        _ctx_1024P = jax.random.normal(jax.random.fold_in(_rk, 11), (8, 16, 256), jnp.float32)
        _ctx_1024c = jax.random.dirichlet(jax.random.fold_in(_rk, 511), 0.3 * jnp.ones((16,), jnp.float32), (8, 375))
        _ctx_1024t = jnp.einsum('bsk,bkd->bsd', _ctx_1024c, _ctx_1024P)
        _ctx_1024t = _ctx_1024t * jax.lax.rsqrt(jnp.mean(jnp.square(_ctx_1024t)) + 1e-12) * 0.953939
        ctx_1024 = -1.39393e-06 + 0.999914 * (_ctx_1024t + 0.3 * jax.random.normal(jax.random.fold_in(_rk, 611), (8, 375, 256), jnp.float32))
        return (x, ctx_1024)
    x, ctx_1024 = _rec_inputs()

    def _L0_xattn_setup():
        import jax, jax.numpy as jnp
        import numpy as np
        D_MODEL = 256
        N_HEADS = 16
        D_K = D_MODEL // N_HEADS
        LN_EPS = 1e-05

        def _attention(query, key_value, W_qkv, b_qkv, W_o, b_o, ln_gamma, ln_beta):
            B, Sq, _ = query.shape
            Skv = key_value.shape[1]
            Wq, Wk, Wv = (W_qkv[:D_MODEL], W_qkv[D_MODEL:2 * D_MODEL], W_qkv[2 * D_MODEL:])
            bq, bk, bv = (b_qkv[:D_MODEL], b_qkv[D_MODEL:2 * D_MODEL], b_qkv[2 * D_MODEL:])
            Q = (query @ Wq.T + bq).reshape(B, Sq, N_HEADS, D_K).transpose(0, 2, 1, 3)
            K = (key_value @ Wk.T + bk).reshape(B, Skv, N_HEADS, D_K).transpose(0, 2, 1, 3)
            V = (key_value @ Wv.T + bv).reshape(B, Skv, N_HEADS, D_K).transpose(0, 2, 1, 3)
            scores = jnp.einsum('bhqd,bhkd->bhqk', Q.astype(jnp.float32), K.astype(jnp.float32))
            scores = scores / np.sqrt(D_K)
            attn = jax.nn.softmax(scores, axis=-1)
            context = jnp.einsum('bhqk,bhkd->bhqd', attn, V.astype(jnp.float32)).astype(query.dtype)
            context = context.transpose(0, 2, 1, 3).reshape(B, Sq, D_MODEL)
            output = context @ W_o.T + b_o
            x = output + query
            mu = jnp.mean(x, axis=-1, keepdims=True)
            var = jnp.mean(jnp.square(x - mu), axis=-1, keepdims=True)
            return (x - mu) / jnp.sqrt(var + LN_EPS) * ln_gamma + ln_beta
        key = jax.random.key(seed)
        ks = jax.random.split(key, 8)
        B, Sq, Skv = (2, 512, 512)
        scale = 1.0 / np.sqrt(D_MODEL)
        return {'query': jax.random.normal(ks[0], (B, Sq, D_MODEL), dtype=jnp.float32), 'key_value': jax.random.normal(ks[1], (B, Skv, D_MODEL), dtype=jnp.float32), 'W_qkv': jax.random.normal(ks[2], (3 * D_MODEL, D_MODEL), dtype=jnp.float32) * scale, 'b_qkv': jax.random.normal(ks[3], (3 * D_MODEL,), dtype=jnp.float32) * 0.01, 'W_o': jax.random.normal(ks[4], (D_MODEL, D_MODEL), dtype=jnp.float32) * scale, 'b_o': jax.random.normal(ks[5], (D_MODEL,), dtype=jnp.float32) * 0.01, 'ln_gamma': jnp.ones((D_MODEL,), dtype=jnp.float32), 'ln_beta': jnp.zeros((D_MODEL,), dtype=jnp.float32)}
    _L0_xattn_all = _L0_xattn_setup()
    _L0_xattn_in = {k: v for k, v in _L0_xattn_all.items() if k in ('W_qkv', 'b_qkv', 'W_o', 'b_o', 'ln_gamma', 'ln_beta')}
    del _L0_xattn_all
    return {'x': x, 'ctx_1024': ctx_1024, 'L0_xattn_W_qkv': _L0_xattn_in['W_qkv'], 'L0_xattn_b_qkv': _L0_xattn_in['b_qkv'], 'L0_xattn_W_o': _L0_xattn_in['W_o'], 'L0_xattn_b_o': _L0_xattn_in['b_o'], 'L0_xattn_ln_gamma': _L0_xattn_in['ln_gamma'], 'L0_xattn_ln_beta': _L0_xattn_in['ln_beta']}

def reference(x, ctx_1024, L0_xattn_W_qkv, L0_xattn_b_qkv, L0_xattn_W_o, L0_xattn_b_o, L0_xattn_ln_gamma, L0_xattn_ln_beta):
    import jax
    import jax.numpy as jnp

    def _L0_xattn_ref(query, key_value, W_qkv, b_qkv, W_o, b_o, ln_gamma, ln_beta):
        import jax, jax.numpy as jnp
        import numpy as np
        D_MODEL = 256
        N_HEADS = 16
        D_K = D_MODEL // N_HEADS
        LN_EPS = 1e-05

        def _attention(query, key_value, W_qkv, b_qkv, W_o, b_o, ln_gamma, ln_beta):
            B, Sq, _ = query.shape
            Skv = key_value.shape[1]
            Wq, Wk, Wv = (W_qkv[:D_MODEL], W_qkv[D_MODEL:2 * D_MODEL], W_qkv[2 * D_MODEL:])
            bq, bk, bv = (b_qkv[:D_MODEL], b_qkv[D_MODEL:2 * D_MODEL], b_qkv[2 * D_MODEL:])
            Q = (query @ Wq.T + bq).reshape(B, Sq, N_HEADS, D_K).transpose(0, 2, 1, 3)
            K = (key_value @ Wk.T + bk).reshape(B, Skv, N_HEADS, D_K).transpose(0, 2, 1, 3)
            V = (key_value @ Wv.T + bv).reshape(B, Skv, N_HEADS, D_K).transpose(0, 2, 1, 3)
            scores = jnp.einsum('bhqd,bhkd->bhqk', Q.astype(jnp.float32), K.astype(jnp.float32))
            scores = scores / np.sqrt(D_K)
            attn = jax.nn.softmax(scores, axis=-1)
            context = jnp.einsum('bhqk,bhkd->bhqd', attn, V.astype(jnp.float32)).astype(query.dtype)
            context = context.transpose(0, 2, 1, 3).reshape(B, Sq, D_MODEL)
            output = context @ W_o.T + b_o
            x = output + query
            mu = jnp.mean(x, axis=-1, keepdims=True)
            var = jnp.mean(jnp.square(x - mu), axis=-1, keepdims=True)
            return (x - mu) / jnp.sqrt(var + LN_EPS) * ln_gamma + ln_beta
        return _attention(query, key_value, W_qkv, b_qkv, W_o, b_o, ln_gamma, ln_beta)
    x = _L0_xattn_ref(x, ctx_1024, L0_xattn_W_qkv, L0_xattn_b_qkv, L0_xattn_W_o, L0_xattn_b_o, L0_xattn_ln_gamma, L0_xattn_ln_beta)
    return x

_drawn_inputs = setup_inputs


def setup_inputs(seed=0):
    import zlib

    import numpy as np

    out = dict(_drawn_inputs(seed))
    spreads = {'L0_xattn_ln_gamma': (1.0, 0.2), 'L0_xattn_ln_beta': (0.0, 0.1)}
    factors = {'L0_xattn_b_qkv': 6.502, 'L0_xattn_b_o': 6.178}
    for name, (base, spread) in spreads.items():
        noise = np.random.default_rng([zlib.crc32(name.encode()), seed]).standard_normal(out[name].shape)
        drawn = base * np.exp(spread * noise) if base else spread * noise
        out[name] = jnp.asarray(drawn.astype(out[name].dtype))
    for name, factor in factors.items():
        out[name] = (out[name] * factor).astype(out[name].dtype)
    return out
```

```python
from contextlib import ExitStack

import numpy as np

import concourse.bass as bass
from concourse import mybir

F32 = mybir.dt.float32
F32R = mybir.dt.float32r
ACT = mybir.ActivationFunctionType
ALU = mybir.AluOpType
AX_X = mybir.AxisListType.X

B, Q, KV, D, H, DK = 8, 112, 375, 256, 16, 16
EPS = 1e-5
PART = 128
EC = D // PART
NC = 3
KC = KV // NC
KVP = KV + 1
NP = H // 2
NG = H // 4
UNITS = NG * NC
GB = 4
QG = GB * Q
VW = DK + 1
SLOT = 16
KROW = NP * KVP
QROW = NP * QG
PRODUCTS = ((0, 0), (0, 1), (1, 0))

M0_JOBS = [("Q", 0, 0), ("K", 0, 0), ("V", 0, 0), ("K", 1, 0), ("Q", 1, 0), ("MT", 0)]
M1_JOBS = [("Q", 0, 1), ("K", 0, 1), ("V", 0, 1), ("K", 1, 1), ("Q", 1, 1), ("BIAS",)]
for _i in range(B + 1):
    if _i + 2 < B:
        M0_JOBS.append(("K", _i + 2, 0))
        M1_JOBS.append(("K", _i + 2, 1))
    if _i + 1 < B:
        M0_JOBS.append(("V", _i + 1, 0))
        M1_JOBS.append(("V", _i + 1, 1))
    if _i >= 1:
        M0_JOBS.append(("OT", _i - 1))
        M1_JOBS.append(("ONT", _i - 1))
        M1_JOBS.append(("OUT", _i - 1))
    if _i + 1 < B:
        M0_JOBS.append(("MT", _i + 1))


def build(nc, x_nat, xT, ctxT, wT, woT, b_cols, bv_cols, b_o, gamma, beta, out):
    q_dram = nc.dram_tensor("q_scratch", (2, 2, 2 * SLOT, QROW), F32, kind="Internal").ap()
    k_dram = nc.dram_tensor("k_scratch", (B, 2, 2 * SLOT, KROW), F32, kind="Internal").ap()

    ctx = ExitStack()
    with ctx:
        def sb(name, shape, dt=F32):
            return ctx.enter_context(nc.sbuf_tensor(name, shape, dt))

        def sem(name):
            return ctx.enter_context(nc.semaphore(name))

        pw = sb("pw", [PART, 4 * GB * Q])
        w_raw = pw[:, 0:EC * 3 * D].rearrange("p (e n) -> p e n", e=EC)
        p_tile = pw[:, :].rearrange("p (r j q) -> p r j q", r=4, j=4)
        w_hl = [sb(f"w_hl{s}", [PART, EC, 3 * D], F32R) for s in range(2)]
        wo = sb("wo", [PART, EC, D])
        x_raw = sb("x_raw", [PART, EC, B * Q])
        k_stack = [sb(f"k_stack{i}", [PART, NP, KVP], F32R) for i in range(2)]
        xk = sb("xk", [PART, 2 * EC * B * Q], F32R)
        x_hl = xk[:, :].rearrange("p (s e n) -> p s e n", s=2, e=EC)
        k_stack.append(xk[:, 0:KROW].rearrange("p (a n) -> p a n", a=NP))
        c_raw = [sb(f"c_raw{i}", [PART, EC, KVP]) for i in range(2)]
        c_hl = [sb(f"c_hl{i}", [PART, 2, EC, KVP], F32R) for i in range(3)]
        k_hl = [sb(f"k_hl{i}", [PART, 2, 2, KVP], F32R) for i in range(2)]
        q_hl = sb("q_hl", [PART, 2, 2, QG], F32R)
        q_stack = sb("q_stack", [PART, 2, NP, GB, 2 * PART], F32R)
        v_sb = [sb(f"v_sb{i}", [PART, NC, H, VW]) for i in range(2)]
        ident = sb("ident", [PART, PART])
        xb = sb("xb", [Q, B, D])
        bqk = sb("bqk", [PART, 4])
        bv = sb("bv", [PART, EC])
        bv_rows = sb("bv_rows", [PART, EC, Q])
        bo_rows = sb("bo_rows", [Q, D])
        g_rows = sb("g_rows", [Q, D])
        be_rows = sb("be_rows", [Q, D])
        mx = [sb(f"mx{i}", [Q, 2, NP]) for i in range(2)]
        neg_m_hi = [sb(f"neg_m_hi{i}", [Q, 2, NP], F32R) for i in range(2)]
        neg_m = [sb(f"neg_m{i}", [Q, 2, 2, NP]) for i in range(2)]
        shift = [sb(f"shift{i}", [2 * 2 * NP, Q], F32R) for i in range(2)]
        o_raw = [sb(f"o_raw{i}", [PART, NG * Q]) for i in range(2)]
        rden = sb("rden", [Q, H, 1])
        o_norm = [sb(f"o_norm{i}", [Q, H, DK]) for i in range(2)]
        o_normT = [sb(f"o_normT{i}", [PART, EC, Q]) for i in range(2)]
        z = [sb(f"z{i}", [Q, D]) for i in range(2)]
        stats = sb("stats", [Q, 6])
        mv = [sb(f"mv{i}", [Q, 2]) for i in range(2)]
        var_eps = sb("var_eps", [Q, 1])
        minus_half = sb("minus_half", [Q, 1])
        rstd = sb("rstd", [Q, 1])
        y = [sb(f"y{i}", [Q, D]) for i in range(2)]
        yo = [sb(f"yo{i}", [Q, D]) for i in range(2)]

        def bank(name):
            return ctx.enter_context(nc.psum_tensor(name, [PART, 512], F32))

        st_bank = [bank(f"st_bank{i}") for i in range(2)]
        mx_bank = [bank(f"mx_bank{i}") for i in range(2)]
        pv_bank = [bank(f"pv_bank{i}") for i in range(2)]
        m_bank = [bank(f"m_bank{i}") for i in range(2)]

        w_in, x_in, bqk_in, const_in = sem("w_in"), sem("x_in"), sem("bqk_in"), sem("const_in")
        c_in = [sem(f"c_in{i}") for i in range(2)]
        q_written, k_written = sem("q_written"), sem("k_written")
        q_in = [sem(f"q_in{g}") for g in range(2)]
        k_in = [sem(f"k_in{i}") for i in range(3)]
        shift_in = [sem(f"shift_in{i}") for i in range(2)]
        stored = [sem(f"stored{i}") for i in range(2)]
        w_hi, w_lo, x_hi, x_lo = sem("w_hi"), sem("w_lo"), sem("x_hi"), sem("x_lo")
        c_hi, c_lo, c_pad = sem("c_hi"), sem("c_lo"), sem("c_pad")
        ident_clear, ident_ready = sem("ident_clear"), sem("ident_ready")
        ones_ready, pv_clear = sem("ones_ready"), sem("pv_clear")
        q_clear = [sem(f"q_clear{g}") for g in range(2)]
        v_ones, bv_ready = sem("v_ones"), sem("bv_ready")
        m_full = [sem(f"m_full{i}") for i in range(2)]
        q_hi, q_lo, k_hi, k_lo = sem("q_hi"), sem("q_lo"), sem("k_hi"), sem("k_lo")
        v_ready = sem("v_ready")
        max_full, max_read = sem("max_full"), sem("max_read")
        neg_hi, neg_ready, shift_ready = sem("neg_hi"), sem("neg_ready"), sem("shift_ready")
        st_full, exp_done, pv_done = sem("st_full"), sem("exp_done"), sem("pv_done")
        o_raw_ready, rden_ready = sem("o_raw_ready"), sem("rden_ready")
        o_norm_ready, o_normT_ready = sem("o_norm_ready"), sem("o_normT_ready")
        bias_ready, xb_ready = sem("bias_ready"), sem("xb_ready")
        z_ready, stats_ready, mv_ready = sem("z_ready"), sem("stats_ready"), sem("mv_ready")
        half_ready, var_ready = sem("half_ready"), sem("var_ready")
        rstd_ready, y_ready, y_scaled, yo_ready = sem("rstd_ready"), sem("y_ready"), sem("y_scaled"), sem("yo_ready")

        CONSTS = 6

        def m_job(*job):
            m = 0 if job in M0_JOBS else 1
            return m, (M0_JOBS, M1_JOBS)[m].index(job)

        last_read = {
            "Q": lambda g, t: (q_lo, 2 * g + t + 1),
            "K": lambda b, t: (k_lo, 2 * b + t + 1),
            "V": lambda b, n: (v_ready, 2 * b + n + 1),
            "BIAS": lambda: (bias_ready, 1),
            "MT": lambda b: (shift_ready, b + 1),
            "OT": lambda b: (o_norm_ready, b + 1),
            "ONT": lambda b: (o_normT_ready, b + 1),
            "OUT": lambda b: (z_ready, b + 1),
        }

        def wait_full(eng, *job):
            m, n = m_job(*job)
            eng.wait_ge(m_full[m], n + 1)
            return m_bank[m]

        block = ctx.enter_context(nc.Block())

        @block.sync
        def _(sp):
            wsrc = wT.rearrange("(e p) n -> p e n", p=PART)
            sp.dma_start(x_raw[:, :, :], xT.rearrange("(e p) n -> p e n", p=PART)).then_inc(x_in, 16)
            sp.dma_start(w_raw, wsrc).then_inc(w_in, 16)

            csrc = ctxT.rearrange("(e p) b n -> p e b n", p=PART)

            def load_context(b):
                if b >= 2:
                    sp.wait_ge(c_lo, b - 1)
                sp.dma_start(c_raw[b % 2][:, :, 0:KV], csrc[:, :, b, :]).then_inc(c_in[b % 2], 16)

            sp.dma_start(bqk[:, :], b_cols).then_inc(bqk_in, 16)
            load_context(0)
            load_context(1)
            sp.dma_start(bv[:, :], bv_cols).then_inc(const_in, 16)
            sp.dma_start(wo[:, :, :], woT.rearrange("(e p) n -> p e n", p=PART)).then_inc(const_in, 16)
            sp.dma_start(xb[:, :, :], x_nat.rearrange("b q d -> q b d")).then_inc(const_in, 16)
            sp.dma_start(bo_rows[:, :], b_o.partition_broadcast(Q)).then_inc(const_in, 16)
            sp.dma_start(g_rows[:, :], gamma.partition_broadcast(Q)).then_inc(const_in, 16)
            sp.dma_start(be_rows[:, :], beta.partition_broadcast(Q)).then_inc(const_in, 16)

            def stack_q(g):
                sp.wait_ge(q_hi, 2 * g + 2)
                sp.wait_ge(q_lo, 2 * g + 2)
                sp.dma_start(q_dram[g].rearrange("s (r4) (p n) -> (r4 p) s n", p=4),
                             q_hl[:, :, :, :].rearrange("r s t n -> r s (t n)").bitcast(F32)).then_inc(q_written, 16)
                sp.wait_ge(q_written, 16 * (g + 1))
                sp.wait_ge(q_clear[g], 2 - g)
                for side in range(2):
                    for slot, part in enumerate((0, 0, 1)):
                        row = 64 * side + SLOT * slot
                        sp.dma_start(
                            q_stack[row:row + SLOT, g, :, :, side * PART:side * PART + Q]
                            .rearrange("d a b q -> d (a b) q").bitcast(F32),
                            q_dram[g, part, side * SLOT:(side + 1) * SLOT, :]
                            .rearrange("d (ab q) -> d ab q", q=Q)).then_inc(q_in[g], 16)

            def stack_k(b):
                sp.wait_ge(k_hi, 2 * b + 2)
                sp.wait_ge(k_lo, 2 * b + 2)
                sp.dma_start(k_dram[b].rearrange("s (r4) (p n) -> (r4 p) s n", p=4),
                             k_hl[b % 2][:, :, :, :].rearrange("r s t n -> r s (t n)").bitcast(F32)).then_inc(k_written, 16)
                sp.wait_ge(k_written, 16 * (b + 1))
                if b >= 3:
                    sp.wait_ge(st_full, UNITS * (b - 2))
                sp.wait_ge(ones_ready, min(b, 2) + 1)
                for side in range(2):
                    row = 64 * side
                    flat = k_stack[b % 3][row:row + 3 * SLOT, :, :].rearrange("r a n -> r (a n)").bitcast(F32)
                    src = k_dram[b, :, side * SLOT:(side + 1) * SLOT, :]
                    sp.dma_start(flat[0:2 * SLOT, :], src).then_inc(k_in[b % 3], 16)
                    sp.dma_start(flat[2 * SLOT:3 * SLOT, :], src[0]).then_inc(k_in[b % 3], 16)

            def stack_shift(b):
                sp.wait_ge(shift_ready, b + 1)
                for side in range(2):
                    row = 64 * side + 3 * SLOT
                    sp.dma_start(q_stack[row:row + 2, b // GB, :, b % GB, side * PART:side * PART + Q]
                                 .bitcast(F32),
                                 shift[b % 2][2 * NP * side:2 * NP * (side + 1), :].bitcast(F32)).then_inc(shift_in[b % 2], 16)

            def store(b):
                sp.wait_ge(yo_ready, b + 1)
                sp.dma_start(out[b], yo[b % 2][:, :]).then_inc(stored[b % 2], 16)

            load_context(2)
            stack_q(0)
            stack_k(0)
            stack_k(1)
            stack_q(1)
            stack_shift(0)
            for i in range(B):
                if i + 3 < B:
                    load_context(i + 3)
                if i + 2 < B:
                    stack_k(i + 2)
                if i + 1 < B:
                    stack_shift(i + 1)
                if i >= 1:
                    store(i - 1)
            store(B - 1)
            for i in range(2):
                sp.wait_ge(stored[i], 16 * (B // 2))

        @block.gpsimd
        def _(pool):
            nc.gpsimd.memset(q_stack[:, 0, 0:NP // 2, :, :].bitcast(F32), 0.0).then_inc(q_clear[0], 1)
            nc.gpsimd.memset(k_stack[0][:, :, :].bitcast(F32), 1.0).then_inc(ones_ready, 1)
            nc.gpsimd.memset(ident[:, :], 0.0).then_inc(ident_clear, 1)
            pool.wait_ge(ident_clear, 1)
            nc.gpsimd.affine_select(out=ident[:, :], in_=ident[:, :], compare_op=ALU.not_equal, fill=1.0,
                                    base=0, pattern=[[-1, PART]], channel_multiplier=1).then_inc(ident_ready, 1)

            def context_lo(b):
                pool.wait_ge(c_hi, b + 1)
                nc.gpsimd.tensor_tensor(c_hl[b % 3][:, 1, :, :], c_raw[b % 2][:, :, :],
                                        c_hl[b % 3][:, 0, :, :].bitcast(F32), op=ALU.subtract).then_inc(c_lo, 1)

            context_lo(0)
            nc.gpsimd.memset(k_stack[1][:, :, :].bitcast(F32), 1.0).then_inc(ones_ready, 1)
            context_lo(1)
            nc.gpsimd.memset(q_stack[:, 1, :, :, :].bitcast(F32), 0.0).then_inc(q_clear[1], 1)
            context_lo(2)
            for t in range(2):
                wait_full(pool, "Q", 1, t)
            nc.gpsimd.memset(k_stack[2].bitcast(F32), 1.0).then_inc(ones_ready, 1)

            pool.wait_ge(bias_ready, 1)
            for b in range(B):
                nc.gpsimd.tensor_tensor(xb[:, b, :], xb[:, b, :], bo_rows[:, :], op=ALU.add).then_inc(xb_ready, 1)

            nc.gpsimd.memset(minus_half[:, :], -0.5).then_inc(half_ready, 1)
            pool.wait_ge(half_ready, 1)

            def inverse_deviation(b):
                pool.wait_ge(mv_ready, b + 1)
                if b >= 1:
                    pool.wait_ge(y_ready, b)
                nc.gpsimd.tensor_scalar(var_eps[:, :], mv[b % 2][:, 1:2], EPS, None,
                                        op0=ALU.add).then_inc(var_ready, 1)
                pool.wait_ge(var_ready, b + 1)
                nc.gpsimd.tensor_tensor(rstd[:, :], var_eps[:, :], minus_half[:, :],
                                        op=ALU.pow).then_inc(rstd_ready, 1)

            def scale_rows(b):
                pool.wait_ge(y_ready, b + 1)
                if b >= 2:
                    pool.wait_ge(stored[b % 2], 16 * (b // 2))
                nc.gpsimd.tensor_tensor(yo[b % 2][:, :], y[b % 2][:, :], g_rows[:, :],
                                        op=ALU.mult).then_inc(y_scaled, 1)
                pool.wait_ge(y_scaled, b + 1)
                nc.gpsimd.tensor_tensor(yo[b % 2][:, :], yo[b % 2][:, :], be_rows[:, :],
                                        op=ALU.add).then_inc(yo_ready, 1)

            for i in range(B + 1):
                if i >= 1:
                    inverse_deviation(i - 1)
                    scale_rows(i - 1)
                if i + 3 < B:
                    context_lo(i + 3)

        @block.scalar
        def _(act):
            act.wait_ge(x_in, 16)
            nc.scalar.copy(x_hl[:, 0, :, :], x_raw[:, :, :]).then_inc(x_hi, 1)
            act.wait_ge(w_in, 16)
            nc.scalar.copy(w_hl[0][:, :, :], w_raw).then_inc(w_hi, 1)
            act.wait_ge(bqk_in, 16)

            def q_hi_part(g, t):
                src = wait_full(act, "Q", g, t)
                if g == 1:
                    act.wait_ge(q_written, 16)
                nc.scalar.activation(q_hl[:, 0, t, :], src[:, 0:QG], ACT.Identity,
                                     bias=bqk[:, t:t + 1]).then_inc(q_hi, 1)

            def k_hi_part(b, t):
                src = wait_full(act, "K", b, t)
                if b >= 2:
                    act.wait_ge(k_written, 16 * (b - 1))
                nc.scalar.activation(k_hl[b % 2][:, 0, t, :], src[:, 0:KVP], ACT.Identity,
                                     bias=bqk[:, 2 + t:3 + t]).then_inc(k_hi, 1)

            def v_part(b, n):
                src = wait_full(act, "V", b, n)
                if b >= 2:
                    act.wait_ge(pv_done, UNITS * (b - 1))
                else:
                    act.wait_ge(v_ones, b + 1)
                c0, chunks = (0, 2) if n == 0 else (2, 1)
                nc.scalar.copy(v_sb[b % 2][0:KC, c0:c0 + chunks, :, 0:DK],
                               src[0:KC, 0:chunks * D].rearrange("p (c h d) -> p c h d", c=chunks, h=H)
                               ).then_inc(v_ready, 1)

            q_hi_part(0, 0)
            q_hi_part(0, 1)
            k_hi_part(0, 0)
            k_hi_part(0, 1)
            v_part(0, 0)
            v_part(0, 1)
            k_hi_part(1, 0)
            k_hi_part(1, 1)
            q_hi_part(1, 0)
            q_hi_part(1, 1)
            act.wait_ge(w_lo, 1)

            def take_o(b):
                act.wait_ge(pv_done, UNITS * (b + 1))
                if b >= 2:
                    m, n = m_job("OT", b - 2)
                    act.wait_ge(m_full[m], n + 1)
                nc.scalar.copy(o_raw[b % 2][:, :], pv_bank[b % 2][:, 0:NG * Q]).then_inc(o_raw_ready, 1)

            def take_o_norm_t(b):
                src = wait_full(act, "ONT", b)
                nc.scalar.copy(o_normT[b % 2][:, :, :],
                               src[:, 0:EC * Q].rearrange("p (k q) -> p k q", k=EC)).then_inc(o_normT_ready, 1)

            for i in range(B):
                for u in range(UNITS):
                    n = UNITS * i + u
                    act.wait_ge(st_full, n + 1)
                    if n >= 4:
                        act.wait_ge(pv_done, n - 3)
                    nc.scalar.activation(
                        p_tile[0:KC, n % 4, :, :],
                        st_bank[n % 2][0:KC, :].rearrange("p (j q) -> p j q", j=4)[:, :, 0:Q],
                        ACT.Exp, scale=float(DK) ** -0.5).then_inc(exp_done, 1)
                    if u < 2 and i + 2 < B:
                        k_hi_part(i + 2, u)
                    if u == 1 and i >= 1:
                        take_o(i - 1)
                    if u in (2, 4) and i + 1 < B:
                        v_part(i + 1, u // 2 - 1)
                    if u == 5 and i >= 1:
                        take_o_norm_t(i - 1)
            take_o(B - 1)
            take_o_norm_t(B - 1)

        @block.vector
        def _(dve):
            nc.vector.memset(q_stack[:, 0, NP // 2:NP, :, :].bitcast(F32), 0.0).then_inc(q_clear[0], 1)
            for i in range(2):
                nc.vector.memset(c_raw[i][:, :, KV:KVP], 0.0).then_inc(c_pad, 1)
                nc.vector.memset(pv_bank[i][:, :], 0.0).then_inc(pv_clear, 1)
                nc.vector.memset(v_sb[i][:, :, :, DK:VW], 1.0).then_inc(v_ones, 1)

            def context_hi(b):
                dve.wait_ge(c_in[b % 2], 16 * (b // 2 + 1))
                if b >= 3:
                    m, n = m_job("V", b - 3, 1)
                    dve.wait_ge(m_full[m], n + 1)
                if b < 2:
                    dve.wait_ge(c_pad, b + 1)
                nc.vector.tensor_copy(c_hl[b % 3][:, 0, :, :], c_raw[b % 2][:, :, :]).then_inc(c_hi, 1)

            dve.wait_ge(x_hi, 1)
            nc.vector.tensor_tensor(x_hl[:, 1, :, :], x_raw[:, :, :], x_hl[:, 0, :, :].bitcast(F32),
                                    op=ALU.subtract).then_inc(x_lo, 1)
            context_hi(0)
            dve.wait_ge(w_hi, 1)
            nc.vector.tensor_tensor(w_hl[1][:, :, :], w_raw, w_hl[0][:, :, :].bitcast(F32),
                                    op=ALU.subtract).then_inc(w_lo, 1)
            context_hi(1)
            dve.wait_ge(bqk_in, 16)

            def q_lo_part(g, t):
                m, _ = m_job("Q", g, t)
                dve.wait_ge(q_hi, 2 * g + t + 1)
                nc.vector.scalar_tensor_tensor(
                    out=q_hl[:, 1, t, :], in0=m_bank[m][:, 0:QG], scalar=bqk[:, t:t + 1],
                    in1=q_hl[:, 0, t, :].bitcast(F32), op0=ALU.add, op1=ALU.subtract).then_inc(q_lo, 1)

            def k_lo_part(b, t):
                m, _ = m_job("K", b, t)
                dve.wait_ge(k_hi, 2 * b + t + 1)
                nc.vector.scalar_tensor_tensor(
                    out=k_hl[b % 2][:, 1, t, :], in0=m_bank[m][:, 0:KVP], scalar=bqk[:, 2 + t:3 + t],
                    in1=k_hl[b % 2][:, 0, t, :].bitcast(F32), op0=ALU.add, op1=ALU.subtract).then_inc(k_lo, 1)

            q_lo_part(0, 0)
            q_lo_part(0, 1)
            k_lo_part(0, 0)
            k_lo_part(0, 1)
            k_lo_part(1, 0)
            k_lo_part(1, 1)
            q_lo_part(1, 0)
            q_lo_part(1, 1)
            context_hi(2)
            dve.wait_ge(const_in, 16 * CONSTS)
            for e in range(EC):
                last = nc.vector.tensor_copy(bv_rows[:, e, :], bv[:, e:e + 1].to_broadcast([PART, Q]))
            last.then_inc(bv_ready, 1)
            src = wait_full(dve, "BIAS")
            nc.vector.tensor_tensor(bo_rows[:, :], src[0:Q, 0:D], bo_rows[:, :], op=ALU.add).then_inc(bias_ready, 1)

            def head_max(b, h):
                n = H * b + h
                dve.wait_ge(max_full, n + 1)
                nc.vector.tensor_reduce(mx[b % 2][:, h % 2, h // 2:h // 2 + 1], mx_bank[n % 2][0:Q, 0:KV],
                                        axis=AX_X, op=ALU.max).then_inc(max_read, 1)

            def negate(b):
                dve.wait_ge(max_read, H * (b + 1))
                nc.vector.tensor_scalar(neg_m_hi[b % 2][:, :, :], mx[b % 2][:, :, :], -1.0, None,
                                        op0=ALU.mult).then_inc(neg_hi, 1)
                dve.wait_ge(neg_hi, 2 * b + 1)
                nc.vector.tensor_copy(neg_m[b % 2][:, :, 0, :],
                                      neg_m_hi[b % 2][:, :, :].bitcast(F32)).then_inc(neg_hi, 1)
                nc.vector.scalar_tensor_tensor(
                    out=neg_m[b % 2][:, :, 1, :], in0=mx[b % 2][:, :, :], scalar=-1.0,
                    in1=neg_m_hi[b % 2][:, :, :].bitcast(F32), op0=ALU.mult, op1=ALU.subtract
                ).then_inc(neg_ready, 1)

            def take_shift(b):
                src = wait_full(dve, "MT", b)
                if b >= 2:
                    dve.wait_ge(shift_in[b % 2], 32 * (b // 2))
                nc.vector.tensor_copy(shift[b % 2][:, :], src[0:2 * 2 * NP, 0:Q]).then_inc(shift_ready, 1)

            def normalise(b):
                src = wait_full(dve, "OT", b)[0:Q, :].rearrange("p (h c) -> p h c", h=H)
                nc.vector.reciprocal(rden[:, :, :], src[:, :, DK:VW]).then_inc(rden_ready, 1)
                dve.wait_ge(rden_ready, b + 1)
                nc.vector.tensor_tensor(o_norm[b % 2][:, :, :], src[:, :, 0:DK],
                                        rden[:, :, :].to_broadcast([Q, H, DK]), op=ALU.mult
                                        ).then_inc(o_norm_ready, 1)

            def layer_norm(b):
                src = wait_full(dve, "OUT", b)
                dve.wait_ge(xb_ready, b + 1)
                nc.vector.tensor_tensor(z[b % 2][:, :], src[0:Q, D:2 * D], xb[:, b, :], op=ALU.add).then_inc(z_ready, 1)
                dve.wait_ge(z_ready, b + 1)
                nc.vector.bn_stats(stats[:, :], z[b % 2][:, :]).then_inc(stats_ready, 1)
                dve.wait_ge(stats_ready, b + 1)
                nc.vector.bn_aggr(mv[b % 2][:, :], stats[:, :]).then_inc(mv_ready, 1)

            def scale_to_norm(b):
                dve.wait_ge(rstd_ready, b + 1)
                if b >= 2:
                    dve.wait_ge(y_scaled, b - 1)
                nc.vector.tensor_scalar(y[b % 2][:, :], z[b % 2][:, :], mv[b % 2][:, 0:1], rstd[:, 0:1], op0=ALU.subtract,
                                        op1=ALU.mult).then_inc(y_ready, 1)

            for h in range(H):
                head_max(0, h)
            negate(0)
            take_shift(0)
            for i in range(B):
                for u in range(UNITS):
                    if u < H // 2 and i + 1 < B:
                        head_max(i + 1, 2 * u)
                        head_max(i + 1, 2 * u + 1)
                    if u < 2 and i + 2 < B:
                        k_lo_part(i + 2, u)
                    if u == 3 and i >= 1:
                        normalise(i - 1)
                    if u == 6 and i >= 1:
                        layer_norm(i - 1)
                    if u == 7 and i >= 1:
                        scale_to_norm(i - 1)
                    if u == 8 and i + 1 < B:
                        negate(i + 1)
                    if u == 9 and i + 1 < B:
                        take_shift(i + 1)
                    if u == 10 and i + 3 < B:
                        context_hi(i + 3)
            normalise(B - 1)
            layer_norm(B - 1)
            scale_to_norm(B - 1)

        @block.tensor
        def _(pe):
            def claim(*job):
                m, n = m_job(*job)
                if n >= 1:
                    kind, *at = (M0_JOBS, M1_JOBS)[m][n - 1]
                    done, count = last_read[kind](*at)
                    pe.wait_ge(done, count)
                return m_bank[m], m_full[m]

            def project(dst, lhs, rhs):
                terms = [(a, c, e) for a, c in PRODUCTS for e in range(EC)]
                for k, (a, c, e) in enumerate(terms):
                    last = nc.tensor.matmul(dst, lhs(a, e), rhs(c, e), start=(k == 0), stop=(k == len(terms) - 1))
                return last

            def q_project(g, t):
                dst, full = claim("Q", g, t)
                project(dst[:, 0:QG], lambda a, e: w_hl[a][:, e, t * PART:(t + 1) * PART],
                        lambda a, e: x_hl[:, a, e, g * QG:(g + 1) * QG]).then_inc(full, 1)

            def k_project(b, t):
                dst, full = claim("K", b, t)
                pe.wait_ge(c_lo, b + 1)
                project(dst[:, 0:KVP], lambda a, e: w_hl[a][:, e, D + t * PART:D + (t + 1) * PART],
                        lambda a, e: c_hl[b % 3][:, a, e, :]).then_inc(full, 1)

            def v_project(b, n):
                dst, full = claim("V", b, n)
                for c in ((0, 1), (2,))[n]:
                    last = project(dst[0:KC, (c % 2) * D:(c % 2 + 1) * D],
                                   lambda a, e: c_hl[b % 3][:, a, e, c * KC:(c + 1) * KC],
                                   lambda a, e: w_hl[a][:, e, 2 * D:3 * D])
                last.then_inc(full, 1)

            def scores_for_max(b, h):
                n = H * b + h
                if n >= 2:
                    pe.wait_ge(max_read, n - 1)
                side = h % 2
                nc.tensor.matmul(mx_bank[n % 2][0:Q, 0:KVP],
                                 q_stack[:, b // GB, h // 2, b % GB, side * PART:side * PART + Q],
                                 k_stack[b % 3][:, h // 2, :], start=True, stop=True).then_inc(max_full, 1)

            def transpose_max(b):
                dst, full = claim("MT", b)
                pe.wait_ge(neg_ready, b + 1)
                nc.tensor.transpose(dst[0:2 * 2 * NP, 0:Q], neg_m[b % 2][:, :, :, :].rearrange("q s l a -> q (s l a)"),
                                    ident[0:Q, 0:Q]).then_inc(full, 1)

            def shifted_scores(i, u):
                n, g, c = UNITS * i + u, u // NC, u % NC
                if u == 0:
                    pe.wait_ge(shift_in[i % 2], 32 * (i // 2 + 1))
                if n >= 2:
                    pe.wait_ge(exp_done, n - 1)
                for k in range(2):
                    last = nc.tensor.matmul(st_bank[n % 2][0:KC, k * 2 * PART:(k + 1) * 2 * PART],
                                            k_stack[i % 3][:, 2 * g + k, c * KC:(c + 1) * KC],
                                            q_stack[:, i // GB, 2 * g + k, i % GB, :], start=True, stop=True)
                last.then_inc(st_full, 1)

            def values(n):
                b, u = n // UNITS, n % UNITS
                g, c = u // NC, u % NC
                pe.wait_ge(exp_done, n + 1)
                if u == 0:
                    pe.wait_ge(v_ready, 2 * b + 2)
                    if b >= 2:
                        pe.wait_ge(o_raw_ready, b - 1)
                for j in range(4):
                    last = nc.tensor.matmul(pv_bank[b % 2][32 * j:32 * j + VW, g * Q:(g + 1) * Q],
                                            v_sb[b % 2][0:KC, c, 4 * g + j, :], p_tile[0:KC, n % 4, j, :],
                                            start=(c == 0), stop=(c == NC - 1))
                last.then_inc(pv_done, 1)

            def transpose_o(b):
                dst, full = claim("OT", b)
                pe.wait_ge(o_raw_ready, b + 1)
                for g in range(NG):
                    last = nc.tensor.transpose(dst[0:Q, g * PART:(g + 1) * PART],
                                               o_raw[b % 2][:, g * Q:(g + 1) * Q], ident[:, :])
                last.then_inc(full, 1)

            def transpose_o_norm(b):
                dst, full = claim("ONT", b)
                pe.wait_ge(o_norm_ready, b + 1)
                flat = o_norm[b % 2][:, :, :].rearrange("q h d -> q (h d)")
                for k in range(EC):
                    last = nc.tensor.transpose(dst[:, k * Q:(k + 1) * Q], flat[:, k * PART:(k + 1) * PART],
                                               ident[0:Q, 0:Q])
                last.then_inc(full, 1)

            def out_project(b):
                dst, full = claim("OUT", b)
                pe.wait_ge(o_normT_ready, b + 1)
                for k in range(EC):
                    last = nc.tensor.matmul(dst[0:Q, D:2 * D], o_normT[b % 2][:, k, :], wo[:, k, :],
                                            start=(k == 0), stop=(k == EC - 1))
                last.then_inc(full, 1)

            pe.wait_ge(x_lo, 1)
            pe.wait_ge(w_lo, 1)
            q_project(0, 0)
            q_project(0, 1)
            k_project(0, 0)
            k_project(0, 1)
            v_project(0, 0)
            v_project(0, 1)
            k_project(1, 0)
            k_project(1, 1)
            q_project(1, 0)
            q_project(1, 1)
            pe.wait_ge(bv_ready, 1)
            dst, full = claim("BIAS")
            for e in range(EC):
                last = nc.tensor.matmul(dst[0:Q, 0:D], bv_rows[:, e, :], wo[:, e, :], start=(e == 0), stop=(e == EC - 1))
            last.then_inc(full, 1)
            pe.wait_ge(q_in[0], 16 * 6)
            pe.wait_ge(k_in[0], 16 * 4)
            for h in range(H):
                scores_for_max(0, h)
            pe.wait_ge(ident_ready, 1)
            pe.wait_ge(pv_clear, 2)
            transpose_max(0)
            for i in range(B):
                for u in range(UNITS):
                    shifted_scores(i, u)
                    if i + u:
                        values(UNITS * i + u - 1)
                    if u < H // 2 and i + 1 < B:
                        if u == 0:
                            pe.wait_ge(k_in[(i + 1) % 3], 64 * ((i + 1) // 3 + 1))
                            if i + 1 == GB:
                                pe.wait_ge(q_in[1], 16 * 6)
                        scores_for_max(i + 1, 2 * u)
                        scores_for_max(i + 1, 2 * u + 1)
                    if u < 2 and i + 2 < B:
                        k_project(i + 2, u)
                    if u in (2, 4) and i + 1 < B:
                        v_project(i + 1, u // 2 - 1)
                    if u == 3 and i >= 1:
                        transpose_o(i - 1)
                    if u == 5 and i >= 1:
                        transpose_o_norm(i - 1)
                    if u == 6 and i >= 1:
                        out_project(i - 1)
                    if u == 9 and i + 1 < B:
                        transpose_max(i + 1)
            values(UNITS * B - 1)
            transpose_o(B - 1)
            transpose_o_norm(B - 1)
            out_project(B - 1)


def by_stack(a):
    rest = a.shape[1:]
    return a.reshape(4, 2, 2, DK, *rest).transpose(1, 2, 3, 0, *range(4, 4 + len(rest))).reshape(D, *rest)


def kernel(x, ctx_1024, L0_xattn_W_qkv, L0_xattn_b_qkv, L0_xattn_W_o, L0_xattn_b_o, L0_xattn_ln_gamma,
           L0_xattn_ln_beta):
    import concourse.bacc as bacc
    from concourse.bass_utils import run_bass_kernel_spmd

    x, ctx_1024, w, b, w_o = (np.asarray(a) for a in (x, ctx_1024, L0_xattn_W_qkv, L0_xattn_b_qkv, L0_xattn_W_o))
    w_rows = np.concatenate([by_stack(w[0:D]), by_stack(w[D:2 * D]), w[2 * D:]])
    b_qk = np.concatenate([by_stack(b[0:D]), by_stack(b[D:2 * D])])
    arrays = {
        "x_nat": x,
        "xT": x.reshape(B * Q, D).T,
        "ctxT": ctx_1024.transpose(2, 0, 1),
        "wT": w_rows.T,
        "woT": w_o.T,
        "b_cols": b_qk.reshape(4, PART).T,
        "bv_cols": b[2 * D:].reshape(EC, PART).T,
        "b_o": np.asarray(L0_xattn_b_o),
        "gamma": np.asarray(L0_xattn_ln_gamma),
        "beta": np.asarray(L0_xattn_ln_beta),
    }
    arrays = {name: np.ascontiguousarray(a) for name, a in arrays.items()}
    nc = bacc.Bacc("TRN2", target_bir_lowering=False, num_devices=1)
    args = [nc.dram_tensor(name, a.shape, mybir.dt.from_np(a.dtype), kind="ExternalInput").ap()
            for name, a in arrays.items()]
    out = nc.dram_tensor("out", (B, Q, D), F32, kind="ExternalOutput").ap()
    build(nc, *args, out)
    return run_bass_kernel_spmd(nc, [arrays], core_ids=[0]).results[0]["out"]
```

```python
from contextlib import ExitStack

import numpy as np

import concourse.bass as bass
from concourse import mybir

F32 = mybir.dt.float32
F32R = mybir.dt.float32r
ACT = mybir.ActivationFunctionType
ALU = mybir.AluOpType
AX_X = mybir.AxisListType.X

B, Q, KV, D, H, DK = 8, 112, 375, 256, 16, 16
EPS = 1e-5
PART = 128
EC = D // PART
NC = 3
KC = KV // NC
KVP = KV + 1
NP = H // 2
NG = H // 4
UNITS = NG * NC
GB = 4
QG = GB * Q
VW = DK + 1
SLOT = 16
KROW = NP * KVP
QROW = NP * GB * PART
PRODUCTS = ((0, 0), (0, 1), (1, 0))

AHEAD = 3
VR = AHEAD + 1
PR = 2 * NC
U_K = (0, 1)
U_OT, U_ONT, U_OUT = 3, 6, 8
U_MT = 7
U_V = (9, 11)

M0_JOBS = [("Q", 0, 0), ("K", 0, 0), ("V", 0, 0), ("K", 1, 0), ("V", 1, 0), ("K", 2, 0), ("Q", 1, 0),
           ("MT", 0), ("V", 2, 0)]
M1_JOBS = [("Q", 0, 1), ("K", 0, 1), ("V", 0, 1), ("K", 1, 1), ("V", 1, 1), ("K", 2, 1), ("Q", 1, 1),
           ("V", 2, 1), ("BIAS",)]
for _i in range(B + 1):
    if _i + AHEAD < B:
        M0_JOBS.append(("K", _i + AHEAD, 0))
        M1_JOBS.append(("K", _i + AHEAD, 1))
    if _i >= 1:
        M0_JOBS.append(("OT", _i - 1))
        M1_JOBS += [("ONT", _i - 1), ("OUT", _i - 1)]
    if _i + 1 < B:
        M0_JOBS.append(("MT", _i + 1))
    if _i + AHEAD < B:
        M0_JOBS.append(("V", _i + AHEAD, 0))
        M1_JOBS.append(("V", _i + AHEAD, 1))

EARLY_HEADS = H + H // 2


def max_heads(n):
    if n < 4:
        return range(EARLY_HEADS + 2 * n, EARLY_HEADS + 2 * n + 2)
    if n < UNITS:
        return range(2 * H + 2 * (n - 4), 2 * H + 2 * (n - 4) + 2)
    m = n - UNITS - 5
    return range(max(0, H * m // UNITS) + 3 * H, min((B - 3) * H, max(0, H * (m + 1) // UNITS)) + 3 * H)


assert [h for n in range(B * UNITS) for h in max_heads(n)] == list(range(EARLY_HEADS, B * H))


def build(nc, x_nat, xT, ctxT, wT, woT, b_cols, bv_cols, b_o, gamma, beta, out):
    q_dram = nc.dram_tensor("q_scratch", (2, 2, 2 * SLOT, QROW), F32, kind="Internal").ap()
    k_dram = nc.dram_tensor("k_scratch", (B, 2, 2 * SLOT, KROW), F32, kind="Internal").ap()

    ctx = ExitStack()
    with ctx:
        def sb(name, shape, dt=F32):
            return ctx.enter_context(nc.sbuf_tensor(name, shape, dt))

        def sem(name):
            return ctx.enter_context(nc.semaphore(name))

        pw = sb("pw", [PART, PR * 4 * Q])
        w_raw = pw[:, 0:EC * 3 * D].rearrange("p (e n) -> p e n", e=EC)
        p_tile = pw[:, :].rearrange("p (r j q) -> p r j q", r=PR, j=4)
        w_hl = [sb(f"w_hl{s}", [PART, EC, 3 * D], F32R) for s in range(2)]
        wo = sb("wo", [PART, EC, D])
        x_raw = sb("x_raw", [PART, EC, B * Q])
        k_stack = [sb(f"k_stack{i}", [PART, NP, KVP], F32R) for i in range(2)]
        xk = sb("xk", [PART, 2 * EC * B * Q], F32R)
        x_hl = xk[:, :].rearrange("p (s e n) -> p s e n", s=2, e=EC)
        k_stack.append(xk[:, 0:KROW].rearrange("p (a n) -> p a n", a=NP))
        c_raw = [sb(f"c_raw{i}", [PART, EC, KVP]) for i in range(2)]
        c_hl = [sb(f"c_hl{i}", [PART, 2, EC, KVP], F32R) for i in range(2)]
        k_hl = [sb(f"k_hl{i}", [PART, 2, 2, KVP], F32R) for i in range(2)]
        q_hl = sb("q_hl", [PART, 2, 2, GB, PART], F32R)
        q_stack = sb("q_stack", [PART, 2, NP, GB, 2 * PART], F32R)
        v_sb = [sb(f"v_sb{i}", [PART, NC, H, VW]) for i in range(VR)]
        ident = sb("ident", [PART, PART])
        one = sb("one", [PART, 1])
        xb = sb("xb", [Q, B, D])
        bqk = sb("bqk", [PART, 4])
        bv = sb("bv", [PART, EC])
        bo_rows = sb("bo_rows", [Q, D])
        g_rows = sb("g_rows", [Q, D])
        be_rows = sb("be_rows", [Q, D])
        mx = [sb(f"mx{i}", [Q, 2, NP]) for i in range(2)]
        neg_m_hi = [sb(f"neg_m_hi{i}", [Q, 2, NP], F32R) for i in range(2)]
        neg_m = [sb(f"neg_m{i}", [Q, 2, 2, NP]) for i in range(2)]
        shift = [sb(f"shift{i}", [2 * 2 * NP, Q], F32R) for i in range(2)]
        o_raw = [sb(f"o_raw{i}", [PART, NG * Q]) for i in range(2)]
        bv_rows = o_raw[0][:, 0:EC * Q].rearrange("p (e q) -> p e q", e=EC)
        rden = sb("rden", [Q, H, 1])
        o_norm = [sb(f"o_norm{i}", [Q, H, DK]) for i in range(2)]
        o_normT = [sb(f"o_normT{i}", [PART, EC, Q]) for i in range(2)]
        z = [sb(f"z{i}", [Q, D]) for i in range(2)]
        stats = sb("stats", [Q, 6])
        mv = [sb(f"mv{i}", [Q, 2]) for i in range(2)]
        var_eps = sb("var_eps", [Q, 1])
        minus_half = sb("minus_half", [Q, 1])
        rstd = sb("rstd", [Q, 1])
        yo = [sb(f"yo{i}", [Q, D]) for i in range(2)]

        def bank(name):
            return ctx.enter_context(nc.psum_tensor(name, [PART, 512], F32))

        st_bank = [bank(f"st_bank{i}") for i in range(2)]
        mx_bank = [bank(f"mx_bank{i}") for i in range(2)]
        pv_bank = [bank(f"pv_bank{i}") for i in range(2)]
        m_bank = [bank(f"m_bank{i}") for i in range(2)]

        bqk_in, const_in = sem("bqk_in"), sem("const_in")
        w_in = [sem(f"w_in{k}") for k in range(3)]
        x_in = [sem(f"x_in{g}") for g in range(2)]
        c_in = [sem(f"c_in{i}") for i in range(2)]
        q_written, k_written = sem("q_written"), sem("k_written")
        q_in = [sem(f"q_in{g}") for g in range(2)]
        k_in = [sem(f"k_in{i}") for i in range(3)]
        shift_in = [sem(f"shift_in{i}") for i in range(2)]
        stored = [sem(f"stored{i}") for i in range(2)]
        w_hi, w_lo, x_hi, x_lo = sem("w_hi"), sem("w_lo"), sem("x_hi"), sem("x_lo")
        c_hi, c_lo, c_pad = sem("c_hi"), sem("c_lo"), sem("c_pad")
        ident_clear, ident_ready = sem("ident_clear"), sem("ident_ready")
        one_ready, q_pad, pv_clear = sem("one_ready"), sem("q_pad"), sem("pv_clear")
        k_ones = [sem(f"k_ones{i}") for i in range(3)]
        q_clear = [sem(f"q_clear{g}") for g in range(2)]
        v_ones, bv_ready = sem("v_ones"), sem("bv_ready")
        m_full = [sem(f"m_full{i}") for i in range(2)]
        q_hi, q_lo, k_hi, k_lo = sem("q_hi"), sem("q_lo"), sem("k_hi"), sem("k_lo")
        v_ready = sem("v_ready")
        max_full, max_read = sem("max_full"), sem("max_read")
        neg_hi, neg_ready, shift_ready = sem("neg_hi"), sem("neg_ready"), sem("shift_ready")
        st_full, exp_done, pv_done = sem("st_full"), sem("exp_done"), sem("pv_done")
        o_raw_ready, rden_ready = sem("o_raw_ready"), sem("rden_ready")
        o_norm_ready, o_normT_ready = sem("o_norm_ready"), sem("o_normT_ready")
        bias_ready, xb_ready = sem("bias_ready"), sem("xb_ready")
        z_ready, stats_ready, mv_ready = sem("z_ready"), sem("stats_ready"), sem("mv_ready")
        half_ready, var_ready = sem("half_ready"), sem("var_ready")
        rstd_ready, y_ready, y_scaled, yo_ready = sem("rstd_ready"), sem("y_ready"), sem("y_scaled"), sem("yo_ready")

        CONSTS = 6

        def m_job(*job):
            m = 0 if job in M0_JOBS else 1
            return m, (M0_JOBS, M1_JOBS)[m].index(job)

        last_read = {
            "Q": lambda g, t: (q_lo, 2 * g + t + 1),
            "K": lambda b, t: (k_lo, 2 * b + t + 1),
            "V": lambda b, n: (v_ready, 2 * b + n + 1),
            "BIAS": lambda: (bias_ready, 1),
            "MT": lambda b: (shift_ready, b + 1),
            "OT": lambda b: (o_norm_ready, b + 1),
            "ONT": lambda b: (o_normT_ready, b + 1),
            "OUT": lambda b: (z_ready, b + 1),
        }

        def wait_full(eng, *job):
            m, n = m_job(*job)
            eng.wait_ge(m_full[m], n + 1)
            return m_bank[m]

        block = ctx.enter_context(nc.Block())

        @block.sync
        def _(sp):
            wsrc = wT.rearrange("(e p) n -> p e n", p=PART)
            xsrc = xT.rearrange("(e p) n -> p e n", p=PART)
            csrc = ctxT.rearrange("(e p) b n -> p e b n", p=PART)

            def load_w(k):
                sp.dma_start(w_raw[:, :, k * D:(k + 1) * D], wsrc[:, :, k * D:(k + 1) * D]).then_inc(w_in[k], 16)

            def load_x(g):
                sp.dma_start(x_raw[:, :, g * QG:(g + 1) * QG], xsrc[:, :, g * QG:(g + 1) * QG]).then_inc(x_in[g], 16)

            def load_context(b):
                if b >= 2:
                    sp.wait_ge(c_lo, b - 1)
                sp.dma_start(c_raw[b % 2][:, :, 0:KV], csrc[:, :, b, :]).then_inc(c_in[b % 2], 16)

            load_x(0)
            load_w(0)
            load_context(0)
            load_w(1)
            sp.dma_start(bqk[:, :], b_cols).then_inc(bqk_in, 16)
            load_w(2)
            load_context(1)
            load_x(1)
            load_context(2)

            def write_q(g):
                sp.wait_ge(q_hi, 2 * g + 2)
                sp.wait_ge(q_lo, 2 * g + 2)
                sp.dma_start(q_dram[g].rearrange("s (r4) (p n) -> (r4 p) s n", p=4),
                             q_hl[:, :, :, :, :].rearrange("r s t b q -> r s (t b q)").bitcast(F32)
                             ).then_inc(q_written, 16)

            def read_q(g):
                sp.wait_ge(q_written, 16 * (g + 1))
                sp.wait_ge(q_clear[g], 2 - g)
                for side in range(2):
                    for slot, part in enumerate((0, 0, 1)):
                        row = 64 * side + SLOT * slot
                        sp.dma_start(
                            q_stack[row:row + SLOT, g, :, :, side * PART:(side + 1) * PART]
                            .rearrange("d a b q -> d (a b) q").bitcast(F32),
                            q_dram[g, part, side * SLOT:(side + 1) * SLOT, :]
                            .rearrange("d (ab q) -> d ab q", q=PART)).then_inc(q_in[g], 16)

            def write_k(b):
                sp.wait_ge(k_hi, 2 * b + 2)
                sp.wait_ge(k_lo, 2 * b + 2)
                sp.dma_start(k_dram[b].rearrange("s (r4) (p n) -> (r4 p) s n", p=4),
                             k_hl[b % 2][:, :, :, :].rearrange("r s t n -> r s (t n)").bitcast(F32)).then_inc(k_written, 16)

            def read_k(b):
                sp.wait_ge(k_written, 16 * (b + 1))
                if b >= 3:
                    sp.wait_ge(st_full, UNITS * (b - 2))
                else:
                    sp.wait_ge(k_ones[b], 1)
                for side in range(2):
                    row = 64 * side
                    flat = k_stack[b % 3][row:row + 3 * SLOT, :, :].rearrange("r a n -> r (a n)").bitcast(F32)
                    src = k_dram[b, :, side * SLOT:(side + 1) * SLOT, :]
                    sp.dma_start(flat[0:2 * SLOT, :], src).then_inc(k_in[b % 3], 16)
                    sp.dma_start(flat[2 * SLOT:3 * SLOT, :], src[0]).then_inc(k_in[b % 3], 16)

            def stack_shift(b):
                sp.wait_ge(shift_ready, b + 1)
                for side in range(2):
                    row = 64 * side + 3 * SLOT
                    sp.dma_start(q_stack[row:row + 2, b // GB, :, b % GB, side * PART:side * PART + Q]
                                 .bitcast(F32),
                                 shift[b % 2][2 * NP * side:2 * NP * (side + 1), :].bitcast(F32)).then_inc(shift_in[b % 2], 16)

            def store(b):
                sp.wait_ge(yo_ready, b + 1)
                sp.dma_start(out[b], yo[b % 2][:, :]).then_inc(stored[b % 2], 16)

            sp.wait_ge(q_pad, 1)
            write_q(0)
            write_k(0)
            read_q(0)
            read_k(0)
            write_k(1)
            load_context(3)
            read_k(1)
            write_k(2)
            stack_shift(0)
            read_k(2)
            write_q(1)
            read_q(1)
            for i in range(B):
                if i + AHEAD - 1 >= AHEAD and i + AHEAD - 1 < B:
                    read_k(i + AHEAD - 1)
                if i + AHEAD < B:
                    write_k(i + AHEAD)
                if i + AHEAD + 1 < B:
                    load_context(i + AHEAD + 1)
                if i + 1 < B:
                    stack_shift(i + 1)
                if i >= 1:
                    store(i - 1)
            store(B - 1)
            for i in range(2):
                sp.wait_ge(stored[i], 16 * (B // 2))

        @block.gpsimd
        def _(pool):
            nc.gpsimd.memset(q_stack[:, 0, 0:NP // 2, :, :].bitcast(F32), 0.0).then_inc(q_clear[0], 1)
            nc.gpsimd.memset(ident[:, :], 0.0).then_inc(ident_clear, 1)
            pool.wait_ge(ident_clear, 1)
            nc.gpsimd.affine_select(out=ident[:, :], in_=ident[:, :], compare_op=ALU.not_equal, fill=1.0,
                                    base=0, pattern=[[-1, PART]], channel_multiplier=1).then_inc(ident_ready, 1)
            nc.gpsimd.memset(minus_half[:, :], -0.5).then_inc(half_ready, 1)

            for tile, source in ((bv, bv_cols), (wo, woT.rearrange("(e p) n -> p e n", p=PART)),
                                 (bo_rows, b_o.partition_broadcast(Q)), (g_rows, gamma.partition_broadcast(Q)),
                                 (be_rows, beta.partition_broadcast(Q))):
                pool.dma_start(tile[:], source).then_inc(const_in, 16)
            nc.gpsimd.memset(q_stack[:, 1, :, :, :].bitcast(F32), 0.0).then_inc(q_clear[1], 1)
            pool.wait_ge(k_in[0], 64)
            pool.dma_start(xb[:, :, :], x_nat.rearrange("b q d -> q b d")).then_inc(const_in, 16)
            for t in range(2):
                wait_full(pool, "Q", 1, t)
            nc.gpsimd.memset(k_stack[2].bitcast(F32), 1.0).then_inc(k_ones[2], 1)

            def context_lo(b):
                pool.wait_ge(c_hi, b + 1)
                nc.gpsimd.tensor_tensor(c_hl[b % 2][:, 1, :, :], c_raw[b % 2][:, :, :],
                                        c_hl[b % 2][:, 0, :, :].bitcast(F32), op=ALU.subtract).then_inc(c_lo, 1)

            context_lo(3)
            pool.wait_ge(bias_ready, 1)
            for b in range(B):
                nc.gpsimd.tensor_tensor(xb[:, b, :], xb[:, b, :], bo_rows[:, :], op=ALU.add).then_inc(xb_ready, 1)

            pool.wait_ge(half_ready, 1)

            def inverse_deviation(b):
                pool.wait_ge(mv_ready, b + 1)
                if b >= 1:
                    pool.wait_ge(y_ready, b)
                nc.gpsimd.tensor_scalar(var_eps[:, :], mv[b % 2][:, 1:2], EPS, None,
                                        op0=ALU.add).then_inc(var_ready, 1)
                pool.wait_ge(var_ready, b + 1)
                nc.gpsimd.tensor_tensor(rstd[:, :], var_eps[:, :], minus_half[:, :],
                                        op=ALU.pow).then_inc(rstd_ready, 1)

            def scale_rows(b):
                pool.wait_ge(y_ready, b + 1)
                if b >= 2:
                    pool.wait_ge(stored[b % 2], 16 * (b // 2))
                nc.gpsimd.tensor_tensor(yo[b % 2][:, :], z[b % 2][:, :], g_rows[:, :],
                                        op=ALU.mult).then_inc(y_scaled, 1)
                pool.wait_ge(y_scaled, b + 1)
                nc.gpsimd.tensor_tensor(yo[b % 2][:, :], yo[b % 2][:, :], be_rows[:, :],
                                        op=ALU.add).then_inc(yo_ready, 1)

            for i in range(B + 1):
                if i >= 1:
                    inverse_deviation(i - 1)
                    scale_rows(i - 1)
                if i + AHEAD + 1 < B:
                    context_lo(i + AHEAD + 1)

        @block.scalar
        def _(act):
            def ones_into(i):
                nc.scalar.copy(k_stack[i][:, :, :].rearrange("p a n -> p (a n)"),
                               one[:, :].to_broadcast([PART, KROW])).then_inc(k_ones[i], 1)

            def x_hi_part(g):
                act.wait_ge(x_in[g], 16)
                nc.scalar.copy(x_hl[:, 0, :, g * QG:(g + 1) * QG], x_raw[:, :, g * QG:(g + 1) * QG]).then_inc(x_hi, 1)

            def w_hi_part(k):
                act.wait_ge(w_in[k], 16)
                nc.scalar.copy(w_hl[0][:, :, k * D:(k + 1) * D], w_raw[:, :, k * D:(k + 1) * D]).then_inc(w_hi, 1)

            def context_hi(b):
                act.wait_ge(c_in[b % 2], 16 * (b // 2 + 1))
                if b < 2:
                    act.wait_ge(c_pad, b + 1)
                else:
                    wait_full(act, "V", b - 2, 1)
                nc.scalar.copy(c_hl[b % 2][:, 0, :, :], c_raw[b % 2][:, :, :]).then_inc(c_hi, 1)

            act.wait_ge(one_ready, 1)
            ones_into(0)
            x_hi_part(0)
            w_hi_part(0)
            context_hi(0)
            w_hi_part(1)
            w_hi_part(2)
            ones_into(1)
            act.wait_ge(bqk_in, 16)

            def q_hi_part(g, t):
                src = wait_full(act, "Q", g, t)
                if g == 1:
                    act.wait_ge(q_written, 16)
                nc.scalar.activation(q_hl[:, 0, t, :, 0:Q], src[:, 0:QG].rearrange("p (b q) -> p b q", b=GB),
                                     ACT.Identity,
                                     bias=bqk[:, t:t + 1]).then_inc(q_hi, 1)

            def k_hi_part(b, t):
                src = wait_full(act, "K", b, t)
                if b >= 2:
                    act.wait_ge(k_written, 16 * (b - 1))
                nc.scalar.activation(k_hl[b % 2][:, 0, t, :], src[:, 0:KVP], ACT.Identity,
                                     bias=bqk[:, 2 + t:3 + t]).then_inc(k_hi, 1)

            def v_part(b, n):
                src = wait_full(act, "V", b, n)
                if b >= VR:
                    act.wait_ge(pv_done, NG * (b - VR + 1))
                else:
                    act.wait_ge(v_ones, b + 1)
                c0, chunks = (0, 2) if n == 0 else (2, 1)
                nc.scalar.copy(v_sb[b % VR][0:KC, c0:c0 + chunks, :, 0:DK],
                               src[0:KC, 0:chunks * D].rearrange("p (c h d) -> p c h d", c=chunks, h=H)
                               ).then_inc(v_ready, 1)

            q_hi_part(0, 0)
            q_hi_part(0, 1)
            context_hi(1)
            for t in range(2):
                k_hi_part(0, t)
            for n in range(2):
                v_part(0, n)
            x_hi_part(1)
            context_hi(2)
            for t in range(2):
                k_hi_part(1, t)
            for n in range(2):
                v_part(1, n)
            for t in range(2):
                k_hi_part(2, t)
            for t in range(2):
                q_hi_part(1, t)
            for n in range(2):
                v_part(2, n)
            act.wait_ge(w_lo, 3)

            def take_o(b):
                act.wait_ge(pv_done, NG * (b + 1))
                if b >= 2:
                    m, n = m_job("OT", b - 2)
                    act.wait_ge(m_full[m], n + 1)
                nc.scalar.copy(o_raw[b % 2][:, :], pv_bank[b % 2][:, 0:NG * Q]).then_inc(o_raw_ready, 1)

            def take_o_norm_t(b):
                src = wait_full(act, "ONT", b)
                nc.scalar.copy(o_normT[b % 2][:, :, :],
                               src[:, 0:EC * Q].rearrange("p (k q) -> p k q", k=EC)).then_inc(o_normT_ready, 1)

            for i in range(B):
                for u in range(UNITS):
                    n = UNITS * i + u
                    act.wait_ge(st_full, n + 1)
                    if n >= PR:
                        act.wait_ge(pv_done, (n - PR) // NC + 1)
                    nc.scalar.activation(
                        p_tile[0:KC, n % PR, :, :],
                        st_bank[n % 2][0:KC, :].rearrange("p (j q) -> p j q", j=4)[:, :, 0:Q],
                        ACT.Exp, scale=float(DK) ** -0.5).then_inc(exp_done, 1)
                    if u == 1 and i >= 1:
                        take_o(i - 1)
                    if u - 1 in U_K and i + AHEAD < B:
                        k_hi_part(i + AHEAD, U_K.index(u - 1))
                    if u - 1 == U_ONT and i >= 1:
                        take_o_norm_t(i - 1)
                    if u - 1 == U_V[0] and i + AHEAD < B:
                        v_part(i + AHEAD, 0)
                    if u == 0 and 1 <= i <= B - AHEAD:
                        v_part(i + AHEAD - 1, 1)
            take_o(B - 1)
            take_o_norm_t(B - 1)

        @block.vector
        def _(dve):
            nc.vector.memset(one[:, :], 1.0).then_inc(one_ready, 1)
            for i in range(2):
                nc.vector.memset(c_raw[i][:, :, KV:KVP], 0.0).then_inc(c_pad, 1)
            nc.vector.memset(q_hl[:, :, :, :, Q:PART].bitcast(F32), 0.0).then_inc(q_pad, 1)
            nc.vector.memset(q_stack[:, 0, NP // 2:NP, :, :].bitcast(F32), 0.0).then_inc(q_clear[0], 1)

            def x_lo_part(g):
                dve.wait_ge(x_hi, g + 1)
                at = slice(g * QG, (g + 1) * QG)
                nc.vector.tensor_tensor(x_hl[:, 1, :, at], x_raw[:, :, at], x_hl[:, 0, :, at].bitcast(F32),
                                        op=ALU.subtract).then_inc(x_lo, 1)

            def w_lo_part(k):
                dve.wait_ge(w_hi, k + 1)
                at = slice(k * D, (k + 1) * D)
                nc.vector.tensor_tensor(w_hl[1][:, :, at], w_raw[:, :, at], w_hl[0][:, :, at].bitcast(F32),
                                        op=ALU.subtract).then_inc(w_lo, 1)

            def context_lo(b):
                dve.wait_ge(c_hi, b + 1)
                nc.vector.tensor_tensor(c_hl[b % 2][:, 1, :, :], c_raw[b % 2][:, :, :],
                                        c_hl[b % 2][:, 0, :, :].bitcast(F32), op=ALU.subtract).then_inc(c_lo, 1)

            def context_hi(b):
                dve.wait_ge(c_in[b % 2], 16 * (b // 2 + 1))
                wait_full(dve, "V", b - 2, 1)
                nc.vector.tensor_copy(c_hl[b % 2][:, 0, :, :], c_raw[b % 2][:, :, :]).then_inc(c_hi, 1)

            x_lo_part(0)
            w_lo_part(0)
            context_lo(0)
            w_lo_part(1)
            w_lo_part(2)
            for i in range(VR):
                nc.vector.memset(v_sb[i][:, :, :, DK:VW], 1.0).then_inc(v_ones, 1)
            for i in range(2):
                nc.vector.memset(pv_bank[i][:, :], 0.0).then_inc(pv_clear, 1)
            dve.wait_ge(bqk_in, 16)

            def q_lo_part(g, t):
                m, _ = m_job("Q", g, t)
                dve.wait_ge(q_hi, 2 * g + t + 1)
                nc.vector.scalar_tensor_tensor(
                    out=q_hl[:, 1, t, :, 0:Q], in0=m_bank[m][:, 0:QG].rearrange("p (b q) -> p b q", b=GB),
                    scalar=bqk[:, t:t + 1], in1=q_hl[:, 0, t, :, 0:Q].bitcast(F32), op0=ALU.add, op1=ALU.subtract).then_inc(q_lo, 1)

            def k_lo_part(b, t):
                m, _ = m_job("K", b, t)
                dve.wait_ge(k_hi, 2 * b + t + 1)
                nc.vector.scalar_tensor_tensor(
                    out=k_hl[b % 2][:, 1, t, :], in0=m_bank[m][:, 0:KVP], scalar=bqk[:, 2 + t:3 + t],
                    in1=k_hl[b % 2][:, 0, t, :].bitcast(F32), op0=ALU.add, op1=ALU.subtract).then_inc(k_lo, 1)

            def bias_rows():
                src = wait_full(dve, "BIAS")
                nc.vector.tensor_tensor(bo_rows[:, :], src[0:Q, 0:D], bo_rows[:, :], op=ALU.add).then_inc(bias_ready, 1)

            q_lo_part(0, 0)
            q_lo_part(0, 1)
            context_lo(1)
            for t in range(2):
                k_lo_part(0, t)
            x_lo_part(1)
            context_lo(2)
            for b in (1, 2):
                for t in range(2):
                    k_lo_part(b, t)
            dve.wait_ge(q_written, 16)
            for t in range(2):
                q_lo_part(1, t)

            def head_max(n):
                b, h = n // H, n % H
                dve.wait_ge(max_full, n + 1)
                nc.vector.tensor_reduce(mx[b % 2][:, h % 2, h // 2:h // 2 + 1], mx_bank[n % 2][0:Q, 0:KV],
                                        axis=AX_X, op=ALU.max).then_inc(max_read, 1)

            def negate(b):
                dve.wait_ge(max_read, H * (b + 1))
                nc.vector.tensor_scalar(neg_m_hi[b % 2][:, :, :], mx[b % 2][:, :, :], -1.0, None,
                                        op0=ALU.mult).then_inc(neg_hi, 1)
                dve.wait_ge(neg_hi, 2 * b + 1)
                nc.vector.tensor_copy(neg_m[b % 2][:, :, 0, :],
                                      neg_m_hi[b % 2][:, :, :].bitcast(F32)).then_inc(neg_hi, 1)
                nc.vector.scalar_tensor_tensor(
                    out=neg_m[b % 2][:, :, 1, :], in0=mx[b % 2][:, :, :], scalar=-1.0,
                    in1=neg_m_hi[b % 2][:, :, :].bitcast(F32), op0=ALU.mult, op1=ALU.subtract
                ).then_inc(neg_ready, 1)

            def take_shift(b):
                src = wait_full(dve, "MT", b)
                if b >= 2:
                    dve.wait_ge(shift_in[b % 2], 32 * (b // 2))
                nc.vector.tensor_copy(shift[b % 2][:, :], src[0:2 * 2 * NP, 0:Q]).then_inc(shift_ready, 1)

            def normalise(b):
                src = wait_full(dve, "OT", b)[0:Q, :].rearrange("p (h c) -> p h c", h=H)
                nc.vector.reciprocal(rden[:, :, :], src[:, :, DK:VW]).then_inc(rden_ready, 1)
                dve.wait_ge(rden_ready, b + 1)
                nc.vector.tensor_tensor(o_norm[b % 2][:, :, :], src[:, :, 0:DK],
                                        rden[:, :, :].to_broadcast([Q, H, DK]), op=ALU.mult
                                        ).then_inc(o_norm_ready, 1)

            def layer_norm(b):
                src = wait_full(dve, "OUT", b)
                dve.wait_ge(xb_ready, b + 1)
                if b >= 2:
                    dve.wait_ge(y_scaled, b - 1)
                nc.vector.tensor_tensor(z[b % 2][:, :], src[0:Q, D:2 * D], xb[:, b, :], op=ALU.add).then_inc(z_ready, 1)
                dve.wait_ge(z_ready, b + 1)
                nc.vector.bn_stats(stats[:, :], z[b % 2][:, :]).then_inc(stats_ready, 1)
                dve.wait_ge(stats_ready, b + 1)
                nc.vector.bn_aggr(mv[b % 2][:, :], stats[:, :]).then_inc(mv_ready, 1)

            def scale_to_norm(b):
                dve.wait_ge(rstd_ready, b + 1)
                nc.vector.tensor_scalar(z[b % 2][:, :], z[b % 2][:, :], mv[b % 2][:, 0:1], rstd[:, 0:1], op0=ALU.subtract,
                                        op1=ALU.mult).then_inc(y_ready, 1)

            for n in range(H):
                head_max(n)
            negate(0)
            for n in range(H, H + 2):
                head_max(n)
            take_shift(0)
            for n in range(H + 2, EARLY_HEADS):
                head_max(n)
            dve.wait_ge(const_in, 16 * CONSTS)
            for e in range(EC):
                last = nc.vector.tensor_copy(bv_rows[:, e, :], bv[:, e:e + 1].to_broadcast([PART, Q]))
            last.then_inc(bv_ready, 1)
            context_hi(3)
            for i in range(B):
                for u in range(UNITS):
                    for n in max_heads(UNITS * i + u):
                        head_max(n)
                    if u - 1 in U_K and i + AHEAD < B:
                        k_lo_part(i + AHEAD, U_K.index(u - 1))
                    if u - 1 == U_OT and i >= 1:
                        normalise(i - 1)
                    if u == U_MT - 1 and i + 1 < B:
                        negate(i + 1)
                    if u - 1 == U_MT and i + 1 < B:
                        take_shift(i + 1)
                    if u - 1 == U_OUT and i >= 1:
                        layer_norm(i - 1)
                    if u == U_OUT + 3 and i >= 1:
                        scale_to_norm(i - 1)
                    if u == U_OUT + 2 and i + AHEAD + 1 < B:
                        context_hi(i + AHEAD + 1)
                    if u == 0 and i == 0:
                        bias_rows()
            normalise(B - 1)
            layer_norm(B - 1)
            scale_to_norm(B - 1)

        @block.tensor
        def _(pe):
            def claim(*job):
                m, n = m_job(*job)
                if n >= 1:
                    kind, *at = (M0_JOBS, M1_JOBS)[m][n - 1]
                    done, count = last_read[kind](*at)
                    pe.wait_ge(done, count)
                return m_bank[m], m_full[m]

            def project(dst, lhs, rhs):
                terms = [(a, c, e) for a, c in PRODUCTS for e in range(EC)]
                for k, (a, c, e) in enumerate(terms):
                    last = nc.tensor.matmul(dst, lhs(a, e), rhs(c, e), start=(k == 0), stop=(k == len(terms) - 1))
                return last

            def q_project(g, t):
                dst, full = claim("Q", g, t)
                pe.wait_ge(x_lo, g + 1)
                pe.wait_ge(w_lo, 1)
                project(dst[:, 0:QG], lambda a, e: w_hl[a][:, e, t * PART:(t + 1) * PART],
                        lambda a, e: x_hl[:, a, e, g * QG:(g + 1) * QG]).then_inc(full, 1)

            def k_project(b, t):
                dst, full = claim("K", b, t)
                pe.wait_ge(c_lo, b + 1)
                pe.wait_ge(w_lo, 2)
                project(dst[:, 0:KVP], lambda a, e: w_hl[a][:, e, D + t * PART:D + (t + 1) * PART],
                        lambda a, e: c_hl[b % 2][:, a, e, :]).then_inc(full, 1)

            def v_project(b, n):
                dst, full = claim("V", b, n)
                pe.wait_ge(w_lo, 3)
                for c in ((0, 1), (2,))[n]:
                    last = project(dst[0:KC, (c % 2) * D:(c % 2 + 1) * D],
                                   lambda a, e: c_hl[b % 2][:, a, e, c * KC:(c + 1) * KC],
                                   lambda a, e: w_hl[a][:, e, 2 * D:3 * D])
                last.then_inc(full, 1)

            def scores_for_max(n):
                b, h = n // H, n % H
                if h == 0:
                    pe.wait_ge(k_in[b % 3], 64 * (b // 3 + 1))
                    if b % GB == 0:
                        pe.wait_ge(q_in[b // GB], 16 * 6)
                if n >= 2:
                    pe.wait_ge(max_read, n - 1)
                side = h % 2
                nc.tensor.matmul(mx_bank[n % 2][0:Q, 0:KVP],
                                 q_stack[:, b // GB, h // 2, b % GB, side * PART:side * PART + Q],
                                 k_stack[b % 3][:, h // 2, :], start=True, stop=True).then_inc(max_full, 1)

            def transpose_max(b):
                dst, full = claim("MT", b)
                pe.wait_ge(neg_ready, b + 1)
                nc.tensor.transpose(dst[0:2 * 2 * NP, 0:Q], neg_m[b % 2][:, :, :, :].rearrange("q s l a -> q (s l a)"),
                                    ident[0:Q, 0:Q]).then_inc(full, 1)

            def shifted_scores(i, u):
                n, g, c = UNITS * i + u, u // NC, u % NC
                if u == 0:
                    pe.wait_ge(shift_in[i % 2], 32 * (i // 2 + 1))
                if n >= 2:
                    pe.wait_ge(exp_done, n - 1)
                for k in range(2):
                    last = nc.tensor.matmul(st_bank[n % 2][0:KC, k * 2 * PART:(k + 1) * 2 * PART],
                                            k_stack[i % 3][:, 2 * g + k, c * KC:(c + 1) * KC],
                                            q_stack[:, i // GB, 2 * g + k, i % GB, :], start=True, stop=True)
                last.then_inc(st_full, 1)

            def values(b, g):
                pe.wait_ge(exp_done, UNITS * b + NC * (g + 1))
                if g == 0:
                    pe.wait_ge(v_ready, 2 * b + 2)
                    if b >= 2:
                        pe.wait_ge(o_raw_ready, b - 1)
                for c in range(NC):
                    for j in range(4):
                        last = nc.tensor.matmul(pv_bank[b % 2][32 * j:32 * j + VW, g * Q:(g + 1) * Q],
                                                v_sb[b % VR][0:KC, c, 4 * g + j, :],
                                                p_tile[0:KC, (UNITS * b + NC * g + c) % PR, j, :],
                                                start=(c == 0), stop=(c == NC - 1))
                last.then_inc(pv_done, 1)

            def transpose_o(b):
                dst, full = claim("OT", b)
                pe.wait_ge(o_raw_ready, b + 1)
                for g in range(NG):
                    last = nc.tensor.transpose(dst[0:Q, g * PART:(g + 1) * PART],
                                               o_raw[b % 2][:, g * Q:(g + 1) * Q], ident[:, :])
                last.then_inc(full, 1)

            def transpose_o_norm(b):
                dst, full = claim("ONT", b)
                pe.wait_ge(o_norm_ready, b + 1)
                flat = o_norm[b % 2][:, :, :].rearrange("q h d -> q (h d)")
                for k in range(EC):
                    last = nc.tensor.transpose(dst[:, k * Q:(k + 1) * Q], flat[:, k * PART:(k + 1) * PART],
                                               ident[0:Q, 0:Q])
                last.then_inc(full, 1)

            def out_project(b):
                dst, full = claim("OUT", b)
                pe.wait_ge(o_normT_ready, b + 1)
                for k in range(EC):
                    last = nc.tensor.matmul(dst[0:Q, D:2 * D], o_normT[b % 2][:, k, :], wo[:, k, :],
                                            start=(k == 0), stop=(k == EC - 1))
                last.then_inc(full, 1)

            q_project(0, 0)
            q_project(0, 1)
            for b in range(2):
                for t in range(2):
                    k_project(b, t)
                for n in range(2):
                    v_project(b, n)
            for t in range(2):
                k_project(2, t)
            for t in range(2):
                q_project(1, t)
            for n in range(H):
                scores_for_max(n)
            pe.wait_ge(ident_ready, 1)
            for n in range(H, H + 2):
                scores_for_max(n)
            transpose_max(0)
            for n in range(H + 2, EARLY_HEADS):
                scores_for_max(n)
            v_project(2, 0)
            v_project(2, 1)
            pe.wait_ge(bv_ready, 1)
            dst, full = claim("BIAS")
            for e in range(EC):
                last = nc.tensor.matmul(dst[0:Q, 0:D], bv_rows[:, e, :], wo[:, e, :], start=(e == 0), stop=(e == EC - 1))
            last.then_inc(full, 1)
            pe.wait_ge(pv_clear, 2)
            for i in range(B):
                for u in range(UNITS):
                    shifted_scores(i, u)
                    for n in max_heads(UNITS * i + u):
                        scores_for_max(n)
                    if u % NC == 0 and i + u:
                        values(*divmod(NG * i + u // NC - 1, NG))
                    if u in U_K and i + AHEAD < B:
                        k_project(i + AHEAD, U_K.index(u))
                    if u == U_OT and i >= 1:
                        transpose_o(i - 1)
                    if u == U_ONT and i >= 1:
                        transpose_o_norm(i - 1)
                    if u == U_MT and i + 1 < B:
                        transpose_max(i + 1)
                    if u == U_OUT and i >= 1:
                        out_project(i - 1)
                    if u in U_V and i + AHEAD < B:
                        v_project(i + AHEAD, U_V.index(u))
            values(B - 1, NG - 1)
            transpose_o(B - 1)
            transpose_o_norm(B - 1)
            out_project(B - 1)


def by_stack(a):
    rest = a.shape[1:]
    return a.reshape(4, 2, 2, DK, *rest).transpose(1, 2, 3, 0, *range(4, 4 + len(rest))).reshape(D, *rest)


def kernel(x, ctx_1024, L0_xattn_W_qkv, L0_xattn_b_qkv, L0_xattn_W_o, L0_xattn_b_o, L0_xattn_ln_gamma,
           L0_xattn_ln_beta):
    import concourse.bacc as bacc
    from concourse.bass_utils import run_bass_kernel_spmd

    x, ctx_1024, w, b, w_o = (np.asarray(a) for a in (x, ctx_1024, L0_xattn_W_qkv, L0_xattn_b_qkv, L0_xattn_W_o))
    w_rows = np.concatenate([by_stack(w[0:D]), by_stack(w[D:2 * D]), w[2 * D:]])
    b_qk = np.concatenate([by_stack(b[0:D]), by_stack(b[D:2 * D])])
    arrays = {
        "x_nat": x,
        "xT": x.reshape(B * Q, D).T,
        "ctxT": ctx_1024.transpose(2, 0, 1),
        "wT": w_rows.T,
        "woT": w_o.T,
        "b_cols": b_qk.reshape(4, PART).T,
        "bv_cols": b[2 * D:].reshape(EC, PART).T,
        "b_o": np.asarray(L0_xattn_b_o),
        "gamma": np.asarray(L0_xattn_ln_gamma),
        "beta": np.asarray(L0_xattn_ln_beta),
    }
    arrays = {name: np.ascontiguousarray(a) for name, a in arrays.items()}
    nc = bacc.Bacc("TRN2", target_bir_lowering=False, num_devices=1)
    args = [nc.dram_tensor(name, a.shape, mybir.dt.from_np(a.dtype), kind="ExternalInput").ap()
            for name, a in arrays.items()]
    out = nc.dram_tensor("out", (B, Q, D), F32, kind="ExternalOutput").ap()
    build(nc, *args, out)
    return run_bass_kernel_spmd(nc, [arrays], core_ids=[0]).results[0]["out"]
```

```python
from contextlib import ExitStack

import numpy as np

import concourse.bass as bass
from concourse import mybir

F32 = mybir.dt.float32
F32R = mybir.dt.float32r
ACT = mybir.ActivationFunctionType
ALU = mybir.AluOpType
AX_X = mybir.AxisListType.X

B, Q, KV, D, H, DK = 8, 112, 375, 256, 16, 16
EPS = 1e-5
PART = 128
EC = D // PART
NC = 3
KC = KV // NC
KVP = KV + 1
NP = H // 2
NG = H // 4
UNITS = NG * NC
GB = 4
QG = GB * Q
VW = DK + 1
SLOT = 16
KROW = NP * KVP
Q_STACKS = ((0, 1), (1, GB), (GB, B))
PRODUCTS = ((0, 0), (0, 1), (1, 0))

AHEAD = 3
VR = AHEAD + 1
PR = 2 * NC
U_K = (0, 2)
U_V = (3, 5, 9)
U_OT, U_ONT, U_OUT = 4, 8, 11
U_NEGATE, U_MT = 4, 7
U_CONTEXT = 6
HEADS = (1, 1, 1, 2, 0, 1, 2, 1, 2, 2, 1, 2)

EARLY_HEADS = H + 6
EARLY_V, EARLY_Q = (2, 4, 6), (9, 12)

M0_JOBS = [("K", 0, 0), ("Q", 0, 0), ("V", 0, 0), ("K", 1, 0), ("V", 1, 0), ("K", 2, 0), ("V", 2, 0),
           ("Q", 1, 0), ("MT", 0)]
M1_JOBS = [("K", 0, 1), ("Q", 0, 1), ("V", 0, 1), ("K", 1, 1), ("V", 1, 1), ("K", 2, 1), ("V", 2, 1),
           ("Q", 1, 1), ("BIAS",)]
for _i in range(B + 1):
    if _i + AHEAD < B:
        M0_JOBS += [("K", _i + AHEAD, 0), ("V", _i + AHEAD, 0)]
        M1_JOBS.append(("K", _i + AHEAD, 1))
    if _i >= 1:
        M1_JOBS += [("OT", _i - 1), ("ONT", _i - 1), ("OUT", _i - 1)]
    if _i + 1 < B:
        M0_JOBS.append(("MT", _i + 1))
    if _i + AHEAD < B:
        M0_JOBS.append(("V", _i + AHEAD, 1))

FIRST_HEADS = (3, 3, 2, 2)
MAX_HEADS = []
for _n in range(B * UNITS):
    _h = MAX_HEADS[-1].stop if MAX_HEADS else EARLY_HEADS
    MAX_HEADS.append(range(_h, min(B * H, _h + (FIRST_HEADS[_n] if _n < len(FIRST_HEADS) else HEADS[_n % UNITS]))))
assert MAX_HEADS[-1].stop == B * H


def build(nc, x_nat, xT, ctxT, wT, woT, b_cols, bv_cols, b_o, gamma, beta, out):
    q_dram = [nc.dram_tensor(f"q_scratch{k}", (2, 2 * SLOT, NP * (b1 - b0) * PART), F32, kind="Internal").ap()
              for k, (b0, b1) in enumerate(Q_STACKS)]
    k_dram = nc.dram_tensor("k_scratch", (B, 2, 2 * SLOT, KROW), F32, kind="Internal").ap()

    ctx = ExitStack()
    with ctx:
        def sb(name, shape, dt=F32):
            return ctx.enter_context(nc.sbuf_tensor(name, shape, dt))

        def sem(name):
            return ctx.enter_context(nc.semaphore(name))

        pw = sb("pw", [PART, PR * 4 * Q])
        w_raw = pw[:, 0:EC * 3 * D].rearrange("p (e n) -> p e n", e=EC)
        p_tile = pw[:, :].rearrange("p (r j q) -> p r j q", r=PR, j=4)
        w_hl = [sb(f"w_hl{s}", [PART, EC, 3 * D], F32R) for s in range(2)]
        wo = sb("wo", [PART, EC, D])
        x_raw = sb("x_raw", [PART, EC, B * Q])
        k_stack = [sb(f"k_stack{i}", [PART, NP, KVP], F32R) for i in range(2)]
        xk = sb("xk", [PART, 2 * EC * B * Q], F32R)
        x_hl = xk[:, :].rearrange("p (s e n) -> p s e n", s=2, e=EC)
        k_stack.append(xk[:, 0:KROW].rearrange("p (a n) -> p a n", a=NP))
        c_raw = [sb(f"c_raw{i}", [PART, EC, KVP]) for i in range(2)]
        c_hl = [sb(f"c_hl{i}", [PART, 2, EC, KVP], F32R) for i in range(2)]
        k_hl = [sb(f"k_hl{i}", [PART, 2, 2, KVP], F32R) for i in range(2)]
        q_hl = sb("q_hl", [PART, 2, 2, GB, PART], F32R)
        q_stack = [sb(f"q_stack{k}", [PART, NP, b1 - b0, 2 * PART], F32R) for k, (b0, b1) in enumerate(Q_STACKS)]
        v_sb = [sb(f"v_sb{i}", [PART, NC, H, VW]) for i in range(VR)]
        ident = sb("ident", [PART, PART])
        xb = sb("xb", [Q, B, D])
        bqk = sb("bqk", [PART, 4])
        bv = sb("bv", [PART, EC])
        bo_rows = sb("bo_rows", [Q, D])
        g_rows = sb("g_rows", [Q, D])
        be_rows = sb("be_rows", [Q, D])
        mx = [sb(f"mx{i}", [Q, 2, NP]) for i in range(2)]
        neg_m_hi = [sb(f"neg_m_hi{i}", [Q, 2, NP], F32R) for i in range(2)]
        neg_m = [sb(f"neg_m{i}", [Q, 2, 2, NP]) for i in range(2)]
        shift = [sb(f"shift{i}", [2 * 2 * NP, Q], F32R) for i in range(2)]
        o_raw = [sb(f"o_raw{i}", [PART, NG * Q]) for i in range(2)]
        bv_rows = o_raw[0][:, 0:EC * Q].rearrange("p (e q) -> p e q", e=EC)
        rden = sb("rden", [Q, H, 1])
        o_norm = [sb(f"o_norm{i}", [Q, H, DK]) for i in range(2)]
        o_normT = [sb(f"o_normT{i}", [PART, EC, Q]) for i in range(2)]
        z = [sb(f"z{i}", [Q, D]) for i in range(2)]
        stats = sb("stats", [Q, 6])
        mv = [sb(f"mv{i}", [Q, 2]) for i in range(2)]
        var_eps = sb("var_eps", [Q, 1])
        minus_half = sb("minus_half", [Q, 1])
        rstd = sb("rstd", [Q, 1])
        yo = [sb(f"yo{i}", [Q, D]) for i in range(2)]

        def bank(name):
            return ctx.enter_context(nc.psum_tensor(name, [PART, 512], F32))

        st_bank = [bank(f"st_bank{i}") for i in range(2)]
        mx_bank = [bank(f"mx_bank{i}") for i in range(2)]
        pv_bank = [bank(f"pv_bank{i}") for i in range(2)]
        m_bank = [bank(f"m_bank{i}") for i in range(2)]

        bqk_in, bv_in, const_in, xb_in = sem("bqk_in"), sem("bv_in"), sem("const_in"), sem("xb_in")
        w_in = [sem(f"w_in{k}") for k in range(3)]
        x_in = [sem(f"x_in{g}") for g in range(2)]
        c_in = [sem(f"c_in{i}") for i in range(2)]
        q_written, k_written = sem("q_written"), sem("k_written")
        q_in = [sem(f"q_in{k}") for k in range(len(Q_STACKS))]
        q_side_in, k_first_in = sem("q_side_in"), sem("k_first_in")
        k_in = [sem(f"k_in{i}") for i in range(3)]
        shift_in = [sem(f"shift_in{i}") for i in range(2)]
        stored = [sem(f"stored{i}") for i in range(2)]
        w_hi, w_lo, x_hi, x_lo = sem("w_hi"), sem("w_lo"), sem("x_hi"), sem("x_lo")
        c_hi, c_lo, c_pad = sem("c_hi"), sem("c_lo"), sem("c_pad")
        ident_clear, ident_ready = sem("ident_clear"), sem("ident_ready")
        q_pad, pv_clear = sem("q_pad"), sem("pv_clear")
        k_ones = [sem(f"k_ones{i}") for i in range(3)]
        q_clear = sem("q_clear")
        v_ones, bv_ready = sem("v_ones"), sem("bv_ready")
        m_full = [sem(f"m_full{i}") for i in range(2)]
        q_hi, q_lo, k_hi, k_lo = sem("q_hi"), sem("q_lo"), sem("k_hi"), sem("k_lo")
        v_ready = sem("v_ready")
        max_full, max_read = sem("max_full"), sem("max_read")
        neg_hi, neg_ready, shift_ready = sem("neg_hi"), sem("neg_ready"), sem("shift_ready")
        st_full, exp_done, pv_done = sem("st_full"), sem("exp_done"), sem("pv_done")
        o_raw_ready, rden_ready = sem("o_raw_ready"), sem("rden_ready")
        o_norm_ready, o_normT_ready = sem("o_norm_ready"), sem("o_normT_ready")
        bias_ready, xb_ready = sem("bias_ready"), sem("xb_ready")
        z_ready, stats_ready, mv_ready = sem("z_ready"), sem("stats_ready"), sem("mv_ready")
        half_ready, var_ready = sem("half_ready"), sem("var_ready")
        last_scaled, last_ready = sem("last_scaled"), sem("last_ready")
        rstd_ready, y_ready, y_scaled, yo_ready = sem("rstd_ready"), sem("y_ready"), sem("y_scaled"), sem("yo_ready")

        W_ORDER = (1, 0, 2)
        SPARSE = UNITS * (B - 2)
        WARM = 4

        def q_stack_of(b):
            return [b0 <= b < b1 for b0, b1 in Q_STACKS].index(True)

        def m_job(*job):
            m = 0 if job in M0_JOBS else 1
            return m, (M0_JOBS, M1_JOBS)[m].index(job)

        last_read = {
            "Q": lambda g, t: (q_lo, 2 * g + t + 1),
            "K": lambda b, t: (k_lo, 2 * b + t + 1),
            "V": lambda b, n: (v_ready, 2 * b + n + 1),
            "BIAS": lambda: (bias_ready, 1),
            "MT": lambda b: (shift_ready, b + 1),
            "OT": lambda b: (o_norm_ready, b + 1),
            "ONT": lambda b: (o_normT_ready, b + 1),
            "OUT": lambda b: (z_ready, b + 1),
        }

        def wait_full(eng, *job):
            m, n = m_job(*job)
            eng.wait_ge(m_full[m], n + 1)
            return m_bank[m]

        def read_q(queue, k, side, arrived):
            queue.wait_ge(q_written, 32 * (k + 1))
            queue.wait_ge(q_clear, k + 1)
            for slot, part in enumerate((0, 0, 1)):
                row = 64 * side + SLOT * slot
                queue.dma_start(
                    q_stack[k][row:row + SLOT, :, :, side * PART:(side + 1) * PART]
                    .rearrange("d a b q -> d (a b) q").bitcast(F32),
                    q_dram[k][part, side * SLOT:(side + 1) * SLOT, :]
                    .rearrange("d (ab q) -> d ab q", q=PART)).then_inc(arrived, 16)

        block = ctx.enter_context(nc.Block())

        @block.sync
        def _(sp):
            wsrc = wT.rearrange("(e p) n -> p e n", p=PART)
            xsrc = xT.rearrange("(e p) n -> p e n", p=PART)
            csrc = ctxT.rearrange("(e p) b n -> p e b n", p=PART)

            def load_w(k):
                sp.dma_start(w_raw[:, :, k * D:(k + 1) * D], wsrc[:, :, k * D:(k + 1) * D]).then_inc(w_in[k], 16)

            def load_x(g):
                sp.dma_start(x_raw[:, :, g * QG:(g + 1) * QG], xsrc[:, :, g * QG:(g + 1) * QG]).then_inc(x_in[g], 16)

            def load_context(b):
                if b >= 2:
                    sp.wait_ge(c_lo, b - 1)
                sp.dma_start(c_raw[b % 2][:, :, 0:KV], csrc[:, :, b, :]).then_inc(c_in[b % 2], 16)

            load_context(0)
            load_w(1)
            sp.dma_start(bqk[:, :], b_cols).then_inc(bqk_in, 16)
            load_x(0)
            load_w(0)
            load_w(2)
            load_context(1)
            load_x(1)
            load_context(2)

            def write_q(k):
                b0, b1 = Q_STACKS[k]
                g, at = b0 // GB, slice(b0 % GB, b0 % GB + b1 - b0)
                sp.wait_ge(q_hi, 2 * g + 2)
                sp.wait_ge(q_lo, 2 * g + 2)
                for t in range(2):
                    sp.dma_start(
                        q_dram[k].rearrange("s (r4) (p t n) -> (r4 p) s t n", p=4, t=2)[:, :, t, :],
                        q_hl[:, :, t, at, :].rearrange("r s b q -> r s (b q)").bitcast(F32)).then_inc(q_written, 16)

            def write_k(b):
                for t in range(2):
                    sp.wait_ge(k_hi, 2 * b + t + 1)
                    sp.wait_ge(k_lo, 2 * b + t + 1)
                    sp.dma_start(k_dram[b].rearrange("s (r4) (p t n) -> (r4 p) s t n", p=4, t=2)[:, :, t, :],
                                 k_hl[b % 2][:, :, t, :].bitcast(F32)).then_inc(k_written, 16)

            def read_k(b, half=None):
                sp.wait_ge(k_written, 32 * (b + 1))
                if b >= 3:
                    sp.wait_ge(st_full, UNITS * (b - 2))
                else:
                    sp.wait_ge(k_ones[b], 1)
                at = slice(0, KROW) if half is None else slice(half * KROW // 2, (half + 1) * KROW // 2)
                arrived = k_first_in if half == 0 else k_in[b % 3]
                for side in range(2):
                    row = 64 * side
                    flat = k_stack[b % 3][row:row + 3 * SLOT, :, :].rearrange("r a n -> r (a n)").bitcast(F32)
                    src = k_dram[b, :, side * SLOT:(side + 1) * SLOT, at]
                    sp.dma_start(flat[0:2 * SLOT, at], src).then_inc(arrived, 16)
                    sp.dma_start(flat[2 * SLOT:3 * SLOT, at], src[0]).then_inc(arrived, 16)

            def stack_shift(b):
                k = q_stack_of(b)
                sp.wait_ge(shift_ready, b + 1)
                for side in range(2):
                    row = 64 * side + 3 * SLOT
                    sp.dma_start(q_stack[k][row:row + 2, :, b - Q_STACKS[k][0], side * PART:side * PART + Q]
                                 .bitcast(F32),
                                 shift[b % 2][2 * NP * side:2 * NP * (side + 1), :].bitcast(F32)).then_inc(shift_in[b % 2], 16)

            def store(b):
                if b < B - 1:
                    sp.wait_ge(yo_ready, b + 1)
                else:
                    sp.wait_ge(last_ready, 1)
                sp.dma_start(out[b], yo[b % 2][:, :]).then_inc(stored[b % 2], 16)

            write_k(0)
            sp.wait_ge(q_pad, 1)
            write_q(0)
            read_k(0, 0)
            read_q(sp, 0, 0, q_in[0])
            read_k(0, 1)
            write_q(1)
            write_k(1)
            load_context(3)
            for side in range(2):
                read_q(sp, 1, side, q_in[1])
            read_k(1)
            write_k(2)
            stack_shift(0)
            read_k(2)
            load_context(4)
            for i in range(B):
                if i + AHEAD + 2 < B:
                    load_context(i + AHEAD + 2)
                if i + AHEAD - 1 >= AHEAD and i + AHEAD - 1 < B:
                    read_k(i + AHEAD - 1)
                if i + AHEAD < B:
                    write_k(i + AHEAD)
                if i >= 2:
                    store(i - 2)
                if i == 0:
                    write_q(2)
                if i == 1:
                    for side in range(2):
                        read_q(sp, 2, side, q_in[2])
                if i + 1 < B:
                    stack_shift(i + 1)
            store(B - 2)
            store(B - 1)
            for i in range(2):
                sp.wait_ge(stored[i], 16 * (B // 2))

        @block.gpsimd
        def _(pool):
            nc.gpsimd.memset(q_stack[0][:].bitcast(F32), 0.0).then_inc(q_clear, 1)
            nc.gpsimd.memset(q_stack[1][:].bitcast(F32), 0.0).then_inc(q_clear, 1)
            nc.gpsimd.memset(k_stack[0][:].bitcast(F32), 1.0).then_inc(k_ones[0], 1)
            nc.gpsimd.memset(ident[:, :], 0.0).then_inc(ident_clear, 1)
            pool.wait_ge(ident_clear, 1)
            nc.gpsimd.affine_select(out=ident[:, :], in_=ident[:, :], compare_op=ALU.not_equal, fill=1.0,
                                    base=0, pattern=[[-1, PART]], channel_multiplier=1).then_inc(ident_ready, 1)
            nc.gpsimd.memset(minus_half[:, :], -0.5).then_inc(half_ready, 1)
            for tile, source in ((bv, bv_cols), (wo, woT.rearrange("(e p) n -> p e n", p=PART))):
                pool.dma_start(tile[:], source).then_inc(bv_in, 16)
            read_q(pool, 0, 1, q_side_in)
            nc.gpsimd.memset(k_stack[1][:].bitcast(F32), 1.0).then_inc(k_ones[1], 1)
            for tile, source in ((bo_rows, b_o), (g_rows, gamma), (be_rows, beta)):
                pool.dma_start(tile[:], source.partition_broadcast(Q)).then_inc(const_in, 16)
            nc.gpsimd.memset(q_stack[2][:].bitcast(F32), 0.0).then_inc(q_clear, 1)
            for t in range(2):
                wait_full(pool, "Q", 1, t)
            nc.gpsimd.memset(k_stack[2].bitcast(F32), 1.0).then_inc(k_ones[2], 1)
            def context_lo(b):
                pool.wait_ge(c_hi, b + 1)
                nc.gpsimd.tensor_tensor(c_hl[b % 2][:, 1, :, :], c_raw[b % 2][:, :, :],
                                        c_hl[b % 2][:, 0, :, :].bitcast(F32), op=ALU.subtract).then_inc(c_lo, 1)

            context_lo(3)
            pool.wait_ge(k_in[2], 64)
            pool.dma_start(xb[:, :, :], x_nat.rearrange("b q d -> q b d")).then_inc(xb_in, 16)

            def bias_into_x():
                pool.wait_ge(bias_ready, 1)
                pool.wait_ge(xb_in, 16)
                for b in range(B):
                    nc.gpsimd.tensor_tensor(xb[:, b, :], xb[:, b, :], bo_rows[:, :], op=ALU.add).then_inc(xb_ready, 1)

            pool.wait_ge(const_in, 48)
            pool.wait_ge(half_ready, 1)

            def inverse_deviation(b):
                pool.wait_ge(mv_ready, b + 1)
                if b >= 1:
                    pool.wait_ge(y_ready, b)
                nc.gpsimd.tensor_scalar(var_eps[:, :], mv[b % 2][:, 1:2], EPS, None,
                                        op0=ALU.add).then_inc(var_ready, 1)
                pool.wait_ge(var_ready, b + 1)
                nc.gpsimd.tensor_tensor(rstd[:, :], var_eps[:, :], minus_half[:, :],
                                        op=ALU.pow).then_inc(rstd_ready, 1)

            def scale_rows(b):
                pool.wait_ge(y_ready, b + 1)
                if b >= 2:
                    pool.wait_ge(stored[b % 2], 16 * (b // 2))
                nc.gpsimd.tensor_tensor(yo[b % 2][:, :], z[b % 2][:, :], g_rows[:, :],
                                        op=ALU.mult).then_inc(y_scaled, 1)
                pool.wait_ge(y_scaled, b + 1)
                nc.gpsimd.tensor_tensor(yo[b % 2][:, :], yo[b % 2][:, :], be_rows[:, :],
                                        op=ALU.add).then_inc(yo_ready, 1)

            for i in range(B + 2):
                if i >= 2:
                    inverse_deviation(i - 2)
                if 2 <= i < B + 1:
                    scale_rows(i - 2)
                if i + AHEAD + 1 < B:
                    context_lo(i + AHEAD + 1)
                if i == 0:
                    bias_into_x()

        @block.scalar
        def _(act):
            def x_hi_part(g):
                act.wait_ge(x_in[g], 16)
                nc.scalar.copy(x_hl[:, 0, :, g * QG:(g + 1) * QG], x_raw[:, :, g * QG:(g + 1) * QG]).then_inc(x_hi, 1)

            def w_hi_part(k):
                act.wait_ge(w_in[k], 16)
                nc.scalar.copy(w_hl[0][:, :, k * D:(k + 1) * D], w_raw[:, :, k * D:(k + 1) * D]).then_inc(w_hi, 1)

            def context_hi(b):
                act.wait_ge(c_in[b % 2], 16 * (b // 2 + 1))
                if b < 2:
                    act.wait_ge(c_pad, b + 1)
                else:
                    wait_full(act, "V", b - 2, 1)
                nc.scalar.copy(c_hl[b % 2][:, 0, :, :], c_raw[b % 2][:, :, :]).then_inc(c_hi, 1)

            def q_hi_part(g, t):
                src = wait_full(act, "Q", g, t)
                if g == 1:
                    act.wait_ge(q_written, 64)
                nc.scalar.activation(q_hl[:, 0, t, :, 0:Q], src[:, 0:QG].rearrange("p (b q) -> p b q", b=GB),
                                     ACT.Identity,
                                     bias=bqk[:, t:t + 1]).then_inc(q_hi, 1)

            def k_hi_part(b, t):
                src = wait_full(act, "K", b, t)
                if b >= 2:
                    act.wait_ge(k_written, 32 * (b - 1))
                nc.scalar.activation(k_hl[b % 2][:, 0, t, :], src[:, 0:KVP], ACT.Identity,
                                     bias=bqk[:, 2 + t:3 + t]).then_inc(k_hi, 1)

            def v_part(b, n):
                src = wait_full(act, "V", b, n)
                if b >= VR:
                    act.wait_ge(pv_done, NG * (b - VR + 1))
                else:
                    act.wait_ge(v_ones, b + 1)
                c0, chunks = (0, 2) if n == 0 else (2, 1)
                nc.scalar.copy(v_sb[b % VR][0:KC, c0:c0 + chunks, :, 0:DK],
                               src[0:KC, 0:chunks * D].rearrange("p (c h d) -> p c h d", c=chunks, h=H)
                               ).then_inc(v_ready, 1)

            context_hi(0)
            w_hi_part(1)
            act.wait_ge(bqk_in, 16)
            x_hi_part(0)
            w_hi_part(0)
            k_hi_part(0, 0)
            k_hi_part(0, 1)
            w_hi_part(2)
            for t in range(2):
                q_hi_part(0, t)
            context_hi(1)
            for n in range(2):
                v_part(0, n)
            for t in range(2):
                k_hi_part(1, t)
            x_hi_part(1)
            context_hi(2)
            for n in range(2):
                v_part(1, n)
            for t in range(2):
                k_hi_part(2, t)
            for n in range(2):
                v_part(2, n)
            for t in range(2):
                q_hi_part(1, t)
            act.wait_ge(w_lo, 3)

            def take_o(b):
                act.wait_ge(pv_done, NG * (b + 1))
                if b >= 2:
                    m, n = m_job("OT", b - 2)
                    act.wait_ge(m_full[m], n + 1)
                nc.scalar.copy(o_raw[b % 2][:, :], pv_bank[b % 2][:, 0:NG * Q]).then_inc(o_raw_ready, 1)

            def take_o_norm_t(b):
                src = wait_full(act, "ONT", b)
                nc.scalar.copy(o_normT[b % 2][:, :, :],
                               src[:, 0:EC * Q].rearrange("p (k q) -> p k q", k=EC)).then_inc(o_normT_ready, 1)

            for i in range(B):
                for u in range(UNITS):
                    n = UNITS * i + u
                    act.wait_ge(st_full, n + 1)
                    if n >= PR:
                        act.wait_ge(pv_done, (n - PR) // NC + 1)
                    nc.scalar.activation(
                        p_tile[0:KC, n % PR, :, :],
                        st_bank[n % 2][0:KC, :].rearrange("p (j q) -> p j q", j=4)[:, :, 0:Q],
                        ACT.Exp, scale=float(DK) ** -0.5).then_inc(exp_done, 1)
                    if u == 2 and i >= 1:
                        take_o(i - 1)
                    if u - 1 in U_K and i + AHEAD < B:
                        k_hi_part(i + AHEAD, U_K.index(u - 1))
                    if u - 1 == U_ONT and i >= 1:
                        take_o_norm_t(i - 1)
                    if u - 1 in U_V[1:] and i + AHEAD < B:
                        v_part(i + AHEAD, U_V[1:].index(u - 1))
            take_o(B - 1)
            take_o_norm_t(B - 1)

        @block.vector
        def _(dve):
            nc.vector.memset(v_sb[0][:, :, :, :], 1.0).then_inc(v_ones, 1)
            for i in range(2):
                nc.vector.memset(c_raw[i][:, :, KV:KVP], 0.0).then_inc(c_pad, 1)
            nc.vector.memset(q_hl[:, :, :, :, Q:PART].bitcast(F32), 0.0).then_inc(q_pad, 1)

            def x_lo_part(g):
                dve.wait_ge(x_hi, g + 1)
                at = slice(g * QG, (g + 1) * QG)
                nc.vector.tensor_tensor(x_hl[:, 1, :, at], x_raw[:, :, at], x_hl[:, 0, :, at].bitcast(F32),
                                        op=ALU.subtract).then_inc(x_lo, 1)

            def w_lo_part(k):
                dve.wait_ge(w_hi, W_ORDER.index(k) + 1)
                at = slice(k * D, (k + 1) * D)
                nc.vector.tensor_tensor(w_hl[1][:, :, at], w_raw[:, :, at], w_hl[0][:, :, at].bitcast(F32),
                                        op=ALU.subtract).then_inc(w_lo, 1)

            def context_lo(b):
                dve.wait_ge(c_hi, b + 1)
                nc.vector.tensor_tensor(c_hl[b % 2][:, 1, :, :], c_raw[b % 2][:, :, :],
                                        c_hl[b % 2][:, 0, :, :].bitcast(F32), op=ALU.subtract).then_inc(c_lo, 1)

            def context_hi(b):
                dve.wait_ge(c_in[b % 2], 16 * (b // 2 + 1))
                wait_full(dve, "V", b - 2, 1)
                nc.vector.tensor_copy(c_hl[b % 2][:, 0, :, :], c_raw[b % 2][:, :, :]).then_inc(c_hi, 1)

            def q_lo_part(g, t):
                m, _ = m_job("Q", g, t)
                dve.wait_ge(q_hi, 2 * g + t + 1)
                nc.vector.scalar_tensor_tensor(
                    out=q_hl[:, 1, t, :, 0:Q], in0=m_bank[m][:, 0:QG].rearrange("p (b q) -> p b q", b=GB),
                    scalar=bqk[:, t:t + 1], in1=q_hl[:, 0, t, :, 0:Q].bitcast(F32), op0=ALU.add, op1=ALU.subtract).then_inc(q_lo, 1)

            def k_lo_part(b, t):
                m, _ = m_job("K", b, t)
                dve.wait_ge(k_hi, 2 * b + t + 1)
                nc.vector.scalar_tensor_tensor(
                    out=k_hl[b % 2][:, 1, t, :], in0=m_bank[m][:, 0:KVP], scalar=bqk[:, 2 + t:3 + t],
                    in1=k_hl[b % 2][:, 0, t, :].bitcast(F32), op0=ALU.add, op1=ALU.subtract).then_inc(k_lo, 1)

            def bias_rows():
                src = wait_full(dve, "BIAS")
                dve.wait_ge(const_in, 48)
                nc.vector.tensor_tensor(bo_rows[:, :], src[0:Q, 0:D], bo_rows[:, :], op=ALU.add).then_inc(bias_ready, 1)

            context_lo(0)
            w_lo_part(1)
            dve.wait_ge(bqk_in, 16)
            x_lo_part(0)
            w_lo_part(0)
            k_lo_part(0, 0)
            k_lo_part(0, 1)
            w_lo_part(2)
            for t in range(2):
                q_lo_part(0, t)
            context_lo(1)
            for i in range(1, VR):
                nc.vector.memset(v_sb[i][:, :, :, DK:VW], 1.0).then_inc(v_ones, 1)
            for t in range(2):
                k_lo_part(1, t)
            x_lo_part(1)
            context_lo(2)
            for i in range(2):
                nc.vector.memset(pv_bank[i][:, :], 0.0).then_inc(pv_clear, 1)
            def head_max(n):
                b, h = n // H, n % H
                dve.wait_ge(max_full, n + 1)
                nc.vector.tensor_reduce(mx[b % 2][:, h % 2, h // 2:h // 2 + 1], mx_bank[n % 2][0:Q, 0:KV],
                                        axis=AX_X, op=ALU.max).then_inc(max_read, 1)

            def negate(b):
                dve.wait_ge(max_read, H * (b + 1))
                nc.vector.tensor_scalar(neg_m_hi[b % 2][:, :, :], mx[b % 2][:, :, :], -1.0, None,
                                        op0=ALU.mult).then_inc(neg_hi, 1)
                dve.wait_ge(neg_hi, 2 * b + 1)
                nc.vector.tensor_copy(neg_m[b % 2][:, :, 0, :],
                                      neg_m_hi[b % 2][:, :, :].bitcast(F32)).then_inc(neg_hi, 1)
                nc.vector.scalar_tensor_tensor(
                    out=neg_m[b % 2][:, :, 1, :], in0=mx[b % 2][:, :, :], scalar=-1.0,
                    in1=neg_m_hi[b % 2][:, :, :].bitcast(F32), op0=ALU.mult, op1=ALU.subtract
                ).then_inc(neg_ready, 1)

            def take_shift(b):
                src = wait_full(dve, "MT", b)
                if b >= 2:
                    dve.wait_ge(shift_in[b % 2], 32 * (b // 2))
                nc.vector.tensor_copy(shift[b % 2][:, :], src[0:2 * 2 * NP, 0:Q]).then_inc(shift_ready, 1)

            def normalise(b):
                src = wait_full(dve, "OT", b)[0:Q, :].rearrange("p (h c) -> p h c", h=H)
                nc.vector.reciprocal(rden[:, :, :], src[:, :, DK:VW]).then_inc(rden_ready, 1)
                dve.wait_ge(rden_ready, b + 1)
                nc.vector.tensor_tensor(o_norm[b % 2][:, :, :], src[:, :, 0:DK],
                                        rden[:, :, :].to_broadcast([Q, H, DK]), op=ALU.mult
                                        ).then_inc(o_norm_ready, 1)

            def layer_norm(b):
                src = wait_full(dve, "OUT", b)
                dve.wait_ge(xb_ready, b + 1)
                if b >= 2:
                    dve.wait_ge(y_scaled, b - 1)
                nc.vector.tensor_tensor(z[b % 2][:, :], src[0:Q, D:2 * D], xb[:, b, :], op=ALU.add).then_inc(z_ready, 1)
                dve.wait_ge(z_ready, b + 1)
                nc.vector.bn_stats(stats[:, :], z[b % 2][:, :]).then_inc(stats_ready, 1)
                dve.wait_ge(stats_ready, b + 1)
                nc.vector.bn_aggr(mv[b % 2][:, :], stats[:, :]).then_inc(mv_ready, 1)

            def scale_to_norm(b):
                dve.wait_ge(rstd_ready, b + 1)
                nc.vector.tensor_scalar(z[b % 2][:, :], z[b % 2][:, :], mv[b % 2][:, 0:1], rstd[:, 0:1], op0=ALU.subtract,
                                        op1=ALU.mult).then_inc(y_ready, 1)

            dve.wait_ge(bv_in, 32)
            for e in range(EC):
                last = nc.vector.tensor_copy(bv_rows[:, e, :], bv[:, e:e + 1].to_broadcast([PART, Q]))
            last.then_inc(bv_ready, 1)
            for t in range(2):
                k_lo_part(2, t)
            for n in range(H):
                head_max(n)
                if n - 1 in EARLY_Q:
                    q_lo_part(1, EARLY_Q.index(n - 1))
            negate(0)
            take_shift(0)
            context_hi(3)
            for n in range(H, EARLY_HEADS):
                head_max(n)
            for i in range(B):
                for u in range(UNITS):
                    heads = MAX_HEADS[UNITS * i + u]
                    for n in heads[:1]:
                        head_max(n)
                    if u - 1 in U_K and i + AHEAD < B:
                        k_lo_part(i + AHEAD, U_K.index(u - 1))
                    if u - 1 == U_OT and i >= 1:
                        normalise(i - 1)
                    if u == U_NEGATE and i + 1 < B:
                        negate(i + 1)
                    if u - 1 == U_MT and i + 1 < B:
                        take_shift(i + 1)
                    if u == 0 and i >= 2:
                        layer_norm(i - 2)
                    if u == 2 and i >= 2:
                        scale_to_norm(i - 2)
                    if u == U_CONTEXT and i + AHEAD + 1 < B:
                        context_hi(i + AHEAD + 1)
                    if u == 0 and i == 0:
                        bias_rows()
                    for n in heads[1:]:
                        head_max(n)
            layer_norm(B - 2)
            normalise(B - 1)
            scale_to_norm(B - 2)
            layer_norm(B - 1)
            scale_to_norm(B - 1)
            b = B - 1
            dve.wait_ge(y_ready, B)
            dve.wait_ge(const_in, 48)
            dve.wait_ge(stored[b % 2], 16 * (b // 2))
            nc.vector.tensor_tensor(yo[b % 2][:, :], z[b % 2][:, :], g_rows[:, :], op=ALU.mult).then_inc(last_scaled, 1)
            dve.wait_ge(last_scaled, 1)
            nc.vector.tensor_tensor(yo[b % 2][:, :], yo[b % 2][:, :], be_rows[:, :], op=ALU.add).then_inc(last_ready, 1)

        @block.tensor
        def _(pe):
            def claim(*job):
                m, n = m_job(*job)
                if n >= 1:
                    kind, *at = (M0_JOBS, M1_JOBS)[m][n - 1]
                    done, count = last_read[kind](*at)
                    pe.wait_ge(done, count)
                return m_bank[m], m_full[m]

            def project(dst, lhs, rhs, hi, rhs_lo, lhs_lo):
                for k, ((a, c), parts) in enumerate(zip(PRODUCTS, (hi, (rhs_lo,), (lhs_lo,)))):
                    for semaphore, count in parts:
                        pe.wait_ge(semaphore, count)
                    for e in range(EC):
                        last = nc.tensor.matmul(dst, lhs(a, e), rhs(c, e), start=(k + e == 0),
                                                stop=(k == len(PRODUCTS) - 1 and e == EC - 1))
                return last

            def w_split(k):
                return W_ORDER.index(k) + 1

            def q_project(g, t):
                dst, full = claim("Q", g, t)
                project(dst[:, 0:QG], lambda a, e: w_hl[a][:, e, t * PART:(t + 1) * PART],
                        lambda a, e: x_hl[:, a, e, g * QG:(g + 1) * QG],
                        ((x_hi, g + 1), (w_hi, w_split(0))), (x_lo, g + 1), (w_lo, w_split(0))).then_inc(full, 1)

            def k_project(b, t):
                dst, full = claim("K", b, t)
                project(dst[:, 0:KVP], lambda a, e: w_hl[a][:, e, D + t * PART:D + (t + 1) * PART],
                        lambda a, e: c_hl[b % 2][:, a, e, :],
                        ((c_hi, b + 1), (w_hi, w_split(1))), (c_lo, b + 1), (w_lo, w_split(1))).then_inc(full, 1)

            def v_project(b, c):
                if c != 1:
                    claim("V", b, c // 2)
                m, _ = m_job("V", b, c // 2)
                last = project(m_bank[m][0:KC, (c % 2) * D:(c % 2 + 1) * D],
                               lambda a, e: c_hl[b % 2][:, a, e, c * KC:(c + 1) * KC],
                               lambda a, e: w_hl[a][:, e, 2 * D:3 * D],
                               ((c_hi, b + 1), (w_hi, w_split(2))), (w_lo, w_split(2)), (c_lo, b + 1))
                if c != 0:
                    last.then_inc(m_full[m], 1)

            def scores_for_max(n):
                b, h = n // H, n % H
                if n == 0:
                    pe.wait_ge(k_first_in, 64)
                if h == 0 and b > 0 or n == H // 2:
                    pe.wait_ge(k_in[b % 3], 64 * (b // 3 + 1))
                k = q_stack_of(b)
                if h == 0 and b == Q_STACKS[k][0]:
                    pe.wait_ge(q_in[k], 16 * (3 if k == 0 else 6))
                if n == 0:
                    pe.wait_ge(q_side_in, 16 * 3)
                if n >= 2:
                    pe.wait_ge(max_read, n - 1)
                side = h % 2
                nc.tensor.matmul(mx_bank[n % 2][0:Q, 0:KVP],
                                 q_stack[k][:, h // 2, b - Q_STACKS[k][0], side * PART:side * PART + Q],
                                 k_stack[b % 3][:, h // 2, :], start=True, stop=True).then_inc(max_full, 1)

            def transpose_max(b):
                dst, full = claim("MT", b)
                pe.wait_ge(neg_ready, b + 1)
                nc.tensor.transpose(dst[0:2 * 2 * NP, 0:Q], neg_m[b % 2][:, :, :, :].rearrange("q s l a -> q (s l a)"),
                                    ident[0:Q, 0:Q]).then_inc(full, 1)

            def shifted_scores(i, u):
                n, g, c = UNITS * i + u, u // NC, u % NC
                qk = q_stack_of(i)
                if u == 0:
                    pe.wait_ge(shift_in[i % 2], 32 * (i // 2 + 1))
                if n >= 2:
                    pe.wait_ge(exp_done, n - 1)
                for k in range(2):
                    last = nc.tensor.matmul(st_bank[n % 2][0:KC, k * 2 * PART:(k + 1) * 2 * PART],
                                            k_stack[i % 3][:, 2 * g + k, c * KC:(c + 1) * KC],
                                            q_stack[qk][:, 2 * g + k, i - Q_STACKS[qk][0], :], start=True, stop=True)
                last.then_inc(st_full, 1)

            def values(b, g, chunks=range(NC)):
                pe.wait_ge(exp_done, UNITS * b + NC * g + chunks[-1] + 1)
                if g == 0 and chunks[0] == 0:
                    pe.wait_ge(v_ready, 2 * b + 2)
                    if b >= 2:
                        pe.wait_ge(o_raw_ready, b - 1)
                for c in chunks:
                    for j in range(4):
                        last = nc.tensor.matmul(pv_bank[b % 2][32 * j:32 * j + VW, g * Q:(g + 1) * Q],
                                                v_sb[b % VR][0:KC, c, 4 * g + j, :],
                                                p_tile[0:KC, (UNITS * b + NC * g + c) % PR, j, :],
                                                start=(c == 0), stop=(c == NC - 1))
                if chunks[-1] == NC - 1:
                    last.then_inc(pv_done, 1)

            def values_of_unit(n):
                values(n // UNITS, n % UNITS // NC, range(n % NC, n % NC + 1))

            def transpose_o(b):
                dst, full = claim("OT", b)
                pe.wait_ge(o_raw_ready, b + 1)
                for g in range(NG):
                    last = nc.tensor.transpose(dst[0:Q, g * PART:(g + 1) * PART],
                                               o_raw[b % 2][:, g * Q:(g + 1) * Q], ident[:, :])
                last.then_inc(full, 1)

            def transpose_o_norm(b):
                dst, full = claim("ONT", b)
                pe.wait_ge(o_norm_ready, b + 1)
                flat = o_norm[b % 2][:, :, :].rearrange("q h d -> q (h d)")
                for k in range(EC):
                    last = nc.tensor.transpose(dst[:, k * Q:(k + 1) * Q], flat[:, k * PART:(k + 1) * PART],
                                               ident[0:Q, 0:Q])
                last.then_inc(full, 1)

            def out_project(b):
                dst, full = claim("OUT", b)
                pe.wait_ge(o_normT_ready, b + 1)
                for k in range(EC):
                    last = nc.tensor.matmul(dst[0:Q, D:2 * D], o_normT[b % 2][:, k, :], wo[:, k, :],
                                            start=(k == 0), stop=(k == EC - 1))
                last.then_inc(full, 1)

            pe.wait_ge(v_ones, 1)
            flat = v_sb[0][:, :, :, :].rearrange("p c h d -> p (c h d)")
            for _ in range(WARM):
                nc.tensor.matmul(mx_bank[0][:, 0:256], flat[:, 0:PART], flat[:, 0:256], start=True, stop=True)
            for t in range(2):
                k_project(0, t)
            for t in range(2):
                q_project(0, t)
            for c in range(NC):
                v_project(0, c)
            for t in range(2):
                k_project(1, t)
            for c in range(NC):
                v_project(1, c)
            for t in range(2):
                k_project(2, t)
            for n in range(H):
                scores_for_max(n)
                if n in EARLY_V:
                    v_project(2, EARLY_V.index(n))
                if n in EARLY_Q:
                    q_project(1, EARLY_Q.index(n))
            pe.wait_ge(bv_ready, 1)
            dst, full = claim("BIAS")
            for e in range(EC):
                last = nc.tensor.matmul(dst[0:Q, 0:D], bv_rows[:, e, :], wo[:, e, :], start=(e == 0), stop=(e == EC - 1))
            last.then_inc(full, 1)
            pe.wait_ge(ident_ready, 1)
            transpose_max(0)
            for n in range(H, EARLY_HEADS):
                scores_for_max(n)
            pe.wait_ge(pv_clear, 2)
            for i in range(B):
                for u in range(UNITS):
                    shifted_scores(i, u)
                    heads = MAX_HEADS[UNITS * i + u]
                    for n in heads[:1]:
                        scores_for_max(n)
                    n = UNITS * i + u
                    if n > SPARSE + 1:
                        values_of_unit(n - 2)
                    elif u % NC == 1 and n > 1:
                        values(*divmod(n // NC - 1, NG))
                    if u in U_K and i + AHEAD < B:
                        k_project(i + AHEAD, U_K.index(u))
                    if u == U_OT and i >= 1:
                        transpose_o(i - 1)
                    if u == U_ONT and i >= 1:
                        transpose_o_norm(i - 1)
                    if u == U_MT and i + 1 < B:
                        transpose_max(i + 1)
                    if u == U_OUT and i >= 1:
                        out_project(i - 1)
                    if u in U_V and i + AHEAD < B:
                        v_project(i + AHEAD, U_V.index(u))
                    for n in heads[1:]:
                        scores_for_max(n)
            for n in (B * UNITS - 2, B * UNITS - 1):
                values_of_unit(n)
            transpose_o(B - 1)
            transpose_o_norm(B - 1)
            out_project(B - 1)


def by_stack(a):
    rest = a.shape[1:]
    return a.reshape(4, 2, 2, DK, *rest).transpose(1, 2, 3, 0, *range(4, 4 + len(rest))).reshape(D, *rest)


def kernel(x, ctx_1024, L0_xattn_W_qkv, L0_xattn_b_qkv, L0_xattn_W_o, L0_xattn_b_o, L0_xattn_ln_gamma,
           L0_xattn_ln_beta):
    import concourse.bacc as bacc
    from concourse.bass_utils import run_bass_kernel_spmd

    x, ctx_1024, w, b, w_o = (np.asarray(a) for a in (x, ctx_1024, L0_xattn_W_qkv, L0_xattn_b_qkv, L0_xattn_W_o))
    w_rows = np.concatenate([by_stack(w[0:D]), by_stack(w[D:2 * D]), w[2 * D:]])
    b_qk = np.concatenate([by_stack(b[0:D]), by_stack(b[D:2 * D])])
    arrays = {
        "x_nat": x,
        "xT": x.reshape(B * Q, D).T,
        "ctxT": ctx_1024.transpose(2, 0, 1),
        "wT": w_rows.T,
        "woT": w_o.T,
        "b_cols": b_qk.reshape(4, PART).T,
        "bv_cols": b[2 * D:].reshape(EC, PART).T,
        "b_o": np.asarray(L0_xattn_b_o),
        "gamma": np.asarray(L0_xattn_ln_gamma),
        "beta": np.asarray(L0_xattn_ln_beta),
    }
    arrays = {name: np.ascontiguousarray(a) for name, a in arrays.items()}
    nc = bacc.Bacc("TRN2", target_bir_lowering=False, num_devices=1)
    args = [nc.dram_tensor(name, a.shape, mybir.dt.from_np(a.dtype), kind="ExternalInput").ap()
            for name, a in arrays.items()]
    out = nc.dram_tensor("out", (B, Q, D), F32, kind="ExternalOutput").ap()
    build(nc, *args, out)
    return run_bass_kernel_spmd(nc, [arrays], core_ids=[0]).results[0]["out"]
```
